# Optimizing a Trainium2 kernel written in Bass

```python
import numpy as np
import jax
import jax.numpy as jnp

def _softmax(x, axis=-1):
    return jax.nn.softmax(x, axis=axis)

def _gelu(x):
    return jax.nn.gelu(x, approximate=True)

def _silu(x):
    return jax.nn.silu(x)

def _sigmoid(x):
    return jax.nn.sigmoid(x)

def _layernorm(x, axis=-1, eps=1e-05):
    m = jnp.mean(x, axis=axis, keepdims=True)
    v = jnp.var(x, axis=axis, keepdims=True)
    return (x - m) / jnp.sqrt(v + eps)

def _scatter_add(tgt, idx, src, axis=0):
    return tgt.at[idx].add(src)

def _segment_sum(src, seg, n):
    return jax.ops.segment_sum(src, seg, n)
kernel_name = 'mk_gnn_preln_d1_gnn_r32_4bff94'

def setup_inputs(seed: int=0):
    np.random.seed(seed)
    _w = jnp.asarray

    def _rec_inputs():
        import jax
        import jax.numpy as jnp
        _gk = jax.random.key(seed)
        x = -1.686e-05 + 1 * jax.random.normal(jax.random.fold_in(_gk, 1), (3125, 160), jnp.float32)
        _s = jax.random.randint(jax.random.fold_in(_gk, 2), (25000,), 0, 3125, jnp.int32)
        _d = jax.random.randint(jax.random.fold_in(_gk, 3), (25000,), 0, 3125, jnp.int32)
        _loop = jnp.arange(3125, dtype=jnp.int32)
        src = jnp.concatenate([_s, _d, _loop])
        dst = jnp.concatenate([_d, _s, _loop])
        _o = jnp.argsort(dst, stable=True)
        src = src[_o]
        dst = dst[_o]
        edge_attr_4 = -0.000107899 + 1.00008 * jax.random.normal(jax.random.fold_in(_gk, 11), (53125, 4), jnp.float32)
        edge_attr_8 = jax.random.uniform(jax.random.fold_in(_gk, 12), (53125, 8), jnp.float32, 0.0, 1)
        return (x, src, dst, edge_attr_4, edge_attr_8)
    x, src, dst, edge_attr_4, edge_attr_8 = _rec_inputs()

    def _L0_gnn_setup():
        import jax, jax.numpy as jnp
        import numpy as np
        N = 50000
        E = 25000
        MUL0 = 64
        MUL1 = 32
        NB = 8
        HID = 64
        WNUM = MUL0 + MUL0 + MUL1 + MUL1
        D_IN = MUL0 + 3 * MUL1
        AVG_DEG = E / N
        key = jax.random.key(seed)
        ks = jax.random.split(key, 16)
        p = lambda i, s: jax.random.normal(ks[i], s, jnp.float32)
        return {'node_features': p(0, (N, D_IN)), 'edge_sh': p(1, (E, 4)), 'edge_embed': jax.random.uniform(ks[2], (E, NB), jnp.float32), 'W1_s': p(3, (MUL0, MUL0)), 'W1_v': p(4, (MUL1, MUL1)), 'fc_w1': p(5, (NB, HID)), 'fc_b1': jnp.zeros((HID,), jnp.float32), 'fc_w2': p(6, (HID, WNUM)) * 0.1, 'fc_b2': jnp.zeros((WNUM,), jnp.float32), 'W2_s': p(7, (96, 96)), 'W2_v': p(8, (96, MUL1)), 'Wsc_s': p(9, (MUL0, 96)), 'Wsc_v': p(10, (MUL1, MUL1)), 'edge_index': jax.random.randint(ks[11], (2, E), 0, N)}
    _L0_gnn_all = _L0_gnn_setup()
    _L0_gnn_in = {k: v for k, v in _L0_gnn_all.items() if k in ('W1_s', 'W1_v', 'fc_w1', 'fc_b1', 'fc_w2', 'fc_b2', 'W2_s', 'W2_v', 'Wsc_s', 'Wsc_v')}
    del _L0_gnn_all
    return {'x': x, 'src': src, 'dst': dst, 'edge_attr_4': edge_attr_4, 'edge_attr_8': edge_attr_8, 'L0_gnn_W1_s': _L0_gnn_in['W1_s'], 'L0_gnn_W1_v': _L0_gnn_in['W1_v'], 'L0_gnn_fc_w1': _L0_gnn_in['fc_w1'], 'L0_gnn_fc_b1': _L0_gnn_in['fc_b1'], 'L0_gnn_fc_w2': _L0_gnn_in['fc_w2'], 'L0_gnn_fc_b2': _L0_gnn_in['fc_b2'], 'L0_gnn_W2_s': _L0_gnn_in['W2_s'], 'L0_gnn_W2_v': _L0_gnn_in['W2_v'], 'L0_gnn_Wsc_s': _L0_gnn_in['Wsc_s'], 'L0_gnn_Wsc_v': _L0_gnn_in['Wsc_v']}

def reference(x, src, dst, edge_attr_4, edge_attr_8, L0_gnn_W1_s, L0_gnn_W1_v, L0_gnn_fc_w1, L0_gnn_fc_b1, L0_gnn_fc_w2, L0_gnn_fc_b2, L0_gnn_W2_s, L0_gnn_W2_v, L0_gnn_Wsc_s, L0_gnn_Wsc_v):
    import jax
    import jax.numpy as jnp

    def _L0_gnn_ref(node_features, edge_sh, edge_embed, W1_s, W1_v, fc_w1, fc_b1, fc_w2, fc_b2, W2_s, W2_v, Wsc_s, Wsc_v, edge_index):
        import jax, jax.numpy as jnp
        import numpy as np
        N = 50000
        E = 25000
        MUL0 = 64
        MUL1 = 32
        NB = 8
        HID = 64
        WNUM = MUL0 + MUL0 + MUL1 + MUL1
        D_IN = MUL0 + 3 * MUL1
        AVG_DEG = E / N
        n = node_features.shape[0]
        s = node_features[:, :MUL0]
        v = node_features[:, MUL0:].reshape(n, MUL1, 3)
        xs = s @ W1_s / np.sqrt(MUL0)
        xv = jnp.einsum('nmc,mk->nkc', v, W1_v) / np.sqrt(MUL1)
        src, dst = (edge_index[0], edge_index[1])
        sh0 = edge_sh[:, 0]
        sh1 = edge_sh[:, 1:4]
        w = jax.nn.silu(edge_embed @ fc_w1 + fc_b1) @ fc_w2 + fc_b2
        w_ss = w[:, :MUL0]
        w_sv = w[:, MUL0:2 * MUL0]
        w_vs = w[:, 2 * MUL0:2 * MUL0 + MUL1]
        w_vv = w[:, 2 * MUL0 + MUL1:]
        xs_e = xs[src]
        xv_e = xv[src]
        m0_a = w_ss * xs_e * sh0[:, None]
        m1_a = (w_sv * xs_e)[:, :, None] * sh1[:, None, :]
        m1_b = w_vs[:, :, None] * xv_e * sh0[:, None, None]
        m0_b = w_vv * jnp.einsum('emc,ec->em', xv_e, sh1) / np.sqrt(3.0)
        msg = jnp.concatenate([m0_a, m0_b, m1_a.reshape(-1, MUL0 * 3), m1_b.reshape(-1, MUL1 * 3)], axis=1)
        agg = jax.ops.segment_sum(msg, dst, num_segments=n) / np.sqrt(AVG_DEG)
        agg_s = agg[:, :96]
        agg_v = agg[:, 96:].reshape(n, 96, 3)
        out_s = agg_s @ W2_s / np.sqrt(96.0)
        out_v = jnp.einsum('nmc,mk->nkc', agg_v, W2_v) / np.sqrt(96.0)
        out_s = out_s + s @ Wsc_s / np.sqrt(MUL0)
        out_v = out_v + jnp.einsum('nmc,mk->nkc', v, Wsc_v) / np.sqrt(MUL1)
        scalars = jax.nn.silu(out_s[:, :MUL0])
        gates = jax.nn.silu(out_s[:, MUL0:MUL0 + MUL1])
        gated = out_v * gates[:, :, None]
        feats = jnp.concatenate([scalars, gated.reshape(n, MUL1 * 3)], axis=1)
        return node_features + feats
    edge_index = jnp.stack([src, dst])
    h = jnp.maximum(_layernorm(x, axis=-1), 0.0)
    x = x + _L0_gnn_ref(h, edge_attr_4, edge_attr_8, L0_gnn_W1_s, L0_gnn_W1_v, L0_gnn_fc_w1, L0_gnn_fc_b1, L0_gnn_fc_w2, L0_gnn_fc_b2, L0_gnn_W2_s, L0_gnn_W2_v, L0_gnn_Wsc_s, L0_gnn_Wsc_v, edge_index)
    return x

_drawn_inputs = setup_inputs


def setup_inputs(seed=0):
    import zlib

    import numpy as np

    out = dict(_drawn_inputs(seed))
    spreads = {'L0_gnn_fc_b1': (0.0, 0.1), 'L0_gnn_fc_b2': (0.0, 0.1)}
    factors = {}
    for name, (base, spread) in spreads.items():
        noise = np.random.default_rng([zlib.crc32(name.encode()), seed]).standard_normal(out[name].shape)
        drawn = base * np.exp(spread * noise) if base else spread * noise
        out[name] = jnp.asarray(drawn.astype(out[name].dtype))
    for name, factor in factors.items():
        out[name] = (out[name] * factor).astype(out[name].dtype)
    return out
```

```python
from contextlib import ExitStack

import concourse.bass as bass
from concourse import mybir

F32 = mybir.dt.float32
I32 = mybir.dt.int32
ALU = mybir.AluOpType
ACT = mybir.ActivationFunctionType
AX = mybir.AxisListType

N = 3125
E = 53125
D = 160
S0, V0, NC = 64, 32, 3
VD = V0 * NC
NB, HID, WN = 8, 64, 192
TE = 128
QT = 4
NQ = -(-E // (TE * QT))
NT = NQ * QT
EP = NT * TE
SLOTS = 4
NI = NQ // SLOTS
WIN = 16
AC = 5
NTN = 125
NN = N // NTN
EPS = 1e-5
assert NI * SLOTS == NQ and NN * NTN == N


def build(nc, x, src_t, dst_t, dst_q, sh_t, emb_t, w1s, w1v, fc1, fb1, fc2, fb2, w2s, w2v, wscs, wscv, out):
    ctx = ExitStack()
    with ctx:
        def sb(name, shape, dt=F32):
            return ctx.enter_context(nc.sbuf_tensor(name, shape, dt))

        def sem(name):
            return ctx.enter_context(nc.semaphore(name))

        x_sb = sb("x_sb", [NTN, NN, D])
        h_sb = sb("h_sb", [NTN, NN, D])
        hT1 = sb("hT1", [128, NN, NTN])
        hT2 = sb("hT2", [V0, NN, NTN])
        stats = sb("stats", [NTN, NN, 6])
        meanvar = sb("meanvar", [NTN, NN, 2])
        rstd = sb("rstd", [NTN, NN])
        nmr = sb("nmr", [NTN, NN])
        eps = sb("eps", [NTN, 1])
        ident = sb("ident", [128, 128])
        tab = sb("tab", [NTN, 5, D])
        wt1 = sb("wt1", [128, D])
        wt2 = sb("wt2", [V0, V0])
        wsc1 = sb("wsc1", [128, WN])
        wsc2 = sb("wsc2", [V0, V0])
        wbc = sb("wbc", [128, WN])
        wa = sb("wa", [128, 96 + V0])
        fc1_sb = sb("fc1_sb", [NB + 1, HID])
        fc2_sb = sb("fc2_sb", [HID + 1, WN])
        src_sb = sb("src_sb", [128, NT], I32)
        dst_sb = sb("dst_sb", [128, NT], I32)
        dstrel = sb("dstrel", [128, NT + QT])
        sh_sb = sb("sh_sb", [128, NT + QT, 4])
        minb = sb("minb", [128, NT])
        iota = sb("iota", [128, WIN, 4])
        dq = sb("dq", [NQ, QT, TE], I32)
        dmin = sb("dmin", [NQ, QT])
        dmax = sb("dmax", [NQ, QT])
        spread = sb("spread", [NQ, QT])
        base = sb("base", [1, NT])
        base_i = sb("base_i", [1, NT], I32)
        spreadrow = sb("spreadrow", [1, NT])
        widest = sb("widest", [1, 1])
        widest_i = sb("widest_i", [1, 1], I32)
        idx = sb("idx", [128, SLOTS, QT], I32)
        gath = sb("gath", [128, SLOTS, QT, D])
        emb = sb("emb", [NB + 1, SLOTS, QT * TE])
        hid = sb("hid", [HID + 1, 2, QT * TE])
        P = sb("P", [128, 2, QT, 2 * D])
        S = sb("S", [128, 2, QT, WIN, 4])
        agg = sb("agg", [128, (N + WIN) * AC])
        act_o = sb("act_o", [NTN, 4, 96])
        res = sb("res", [NTN, 4, D])

        ps = ctx.enter_context(nc.psum_tensor("ps", [128, 8, 512], F32))
        table = nc.dram_tensor("table", [N, D], F32, kind="Internal").ap()
        dmin_d = nc.dram_tensor("dmin_d", [NQ, QT], F32, kind="Internal").ap()
        spread_d = nc.dram_tensor("spread_d", [NQ, QT], F32, kind="Internal").ap()

        agg_v = agg[:, 0:N * AC].rearrange("p (n c) -> p n c", c=AC)
        xv = x.rearrange("(t p) d -> p t d", p=NTN)
        outv = out.rearrange("(t p) d -> t p d", p=NTN)

        def vec(ap):
            return ap.rearrange("p (m c) -> p c m", c=NC)

        s_x, s_emb0, s_idx, s_dq, s_w, s_zero = (sem("s_" + n) for n in ("x", "emb0", "idx", "dq", "w", "zero"))
        s_eps, s_ident, s_iota, s_ones = (sem("s_" + n) for n in ("eps", "ident", "iota", "ones"))
        s_stat, s_std, s_rstd, s_h, s_hT, s_hTsb = (sem("s_" + n) for n in ("stat", "std", "rstd", "h", "hT", "hTsb"))
        s_tabps, s_tabsb, s_scaled, s_dve = (sem("s_" + n) for n in ("tabps", "tabsb", "scaled", "dve"))
        s_tabw = [sem(f"s_tabw{i}") for i in range(5)]
        s_mm, s_mmout, s_mmb, s_mmrow, s_spread = (sem("s_" + n) for n in ("mm", "mmout", "mmb", "mmrow", "spread"))
        WZERO = 4
        wloads = [
            (wt1[0:S0, 0:S0], w1s), (wt1[64:96, 64:96], w1v), (wt1[96:128, 96:128], w1v), (wt2[:, :], w1v),
            (wsc1[0:S0, 0:96], wscs), (wsc1[64:96, 96:128], wscv), (wsc1[96:128, 128:160], wscv), (wsc2[:, :], wscv),
            (wa[0:S0, 0:96], w2s[0:S0, :]), (wa[64:128, 96:96 + V0], w2v[0:S0, :]),
            (wbc[0:32, 96:128], w2v[S0:96, :]), (wbc[32:64, 128:160], w2v[S0:96, :]),
            (wbc[64:96, 160:192], w2v[S0:96, :]), (wbc[96:128, 0:96], w2s[S0:96, :]),
            (fc1_sb[0:NB, :], fc1), (fc1_sb[NB:NB + 1, :], fb1),
            (fc2_sb[0:HID, :], fc2), (fc2_sb[HID:HID + 1, :], fb2),
        ]
        WIDE = [(0, 2), (2, 4)]

        with nc.Block() as block:
            @block.sync
            def _(sp):
                sp.dma_start(x_sb[:, 0:NN, :], xv).then_inc(s_x, 16)
                sp.wait_ge(s_zero, 1)
                for dst, w in wloads:
                    sp.dma_start(dst, w).then_inc(s_w, 16)
                for t in range(NN):
                    sp.wait_ge(s_tabsb, t + 1)
                    sp.dma_start(table[t * NTN:(t + 1) * NTN, :], tab[:, t % 5, :]).then_inc(s_tabw[t % 5], 16)
                for i in range(5):
                    sp.wait_ge(s_tabw[i], 16 * 5)

            @block.gpsimd
            def _(pool):
                nc.gpsimd.memset(ident[:, :], 0.0).then_inc(s_ident, 1)
                pool.wait_ge(s_ident, 1)
                nc.gpsimd.affine_select(out=ident[:, :], in_=ident[:, :], compare_op=ALU.not_equal, fill=1.0, base=0,
                                        pattern=[[-1, 128]], channel_multiplier=1).then_inc(s_ident, 1)
                nc.gpsimd.iota(iota[:, :, :], pattern=[[1, WIN], [0, 4]], base=0, channel_multiplier=0,
                               allow_small_or_imprecise_dtypes=True).then_inc(s_iota, 1)
                nc.gpsimd.memset(hid[:, :, :], 1.0)
                nc.gpsimd.memset(emb[:, :, :], 1.0)
                nc.gpsimd.memset(agg[:, :], 0.0).then_inc(s_ones, 1)
                pool.wait_ge(s_iota, 1)
                pool.wait_ge(s_ones, 1)

            @block.scalar
            def _(act):
                def table_rows(t):
                    act.wait_ge(s_tabps, t + 1)
                    if t >= 5:
                        act.wait_ge(s_tabw[t % 5], 16 * (t // 5))
                    nc.scalar.copy(tab[:, t % 5, :], ps[0:NTN, 4 + t % 2, 0:D]).then_inc(s_tabsb, 1)

                act.dma_start(dq[:, :, :], dst_q).then_inc(s_dq, 16)
                act.dma_start(src_sb[:, :], src_t).then_inc(s_idx, 16)
                act.dma_start(dst_sb[:, :], dst_t).then_inc(s_idx, 16)
                act.dma_start(sh_sb[:, :, :], sh_t).then_inc(s_idx, 16)
                act.wait_ge(s_mm, 1)
                act.dma_start(dmin_d, dmin[:, :]).then_inc(s_mmout, 16)
                act.dma_start(spread_d, spread[:, :]).then_inc(s_mmout, 16)
                act.wait_ge(s_mmout, 32)
                flat = dmin_d.rearrange("q t -> (q t)").unsqueeze(0)
                act.dma_start(minb[:, :], flat.broadcast_to([128, NT])).then_inc(s_mmb, 16)
                act.dma_start(base[:, :], flat).then_inc(s_mmb, 16)
                act.dma_start(spreadrow[:, :], spread_d.rearrange("q t -> (q t)").unsqueeze(0)).then_inc(s_mmb, 16)
                act.wait_ge(s_eps, 1)
                for t in range(NN):
                    if t % 5 == 0:
                        act.wait_ge(s_stat, t // 5 + 1)
                        nc.scalar.activation(rstd[:, t:t + 5], meanvar[:, t:t + 5, 1], ACT.Sqrt,
                                             bias=eps[:, 0:1]).then_inc(s_std, 1)
                        act.wait_ge(s_rstd, t // 5 + 1)
                    r, m = rstd[:, t:t + 1], nmr[:, t:t + 1]
                    nc.scalar.activation(h_sb[:, t, 0:S0], x_sb[:, t, 0:S0], ACT.Relu, bias=m, scale=r)
                    nc.scalar.activation(h_sb[:, t, S0:D].rearrange("p (c m) -> p c m", c=NC), vec(x_sb[:, t, S0:D]),
                                         ACT.Relu, bias=m, scale=r).then_inc(s_h, 1)
                    if t >= 5:
                        table_rows(t - 5)
                for t in range(NN - 5, NN):
                    table_rows(t)

            @block.vector
            def _(dve):
                def h_columns(t):
                    dve.wait_ge(s_hT, t + 1)
                    nc.vector.tensor_copy(hT1[:, t, :], ps[:, t % 2, 0:NTN])
                    nc.vector.tensor_copy(hT2[:, t, :], ps[0:V0, 2 + t % 2, 0:NTN]).then_inc(s_hTsb, 1)

                chain = [0]

                def link(ins):
                    chain[0] += 1
                    ins.then_inc(s_dve, 1)
                    dve.wait_ge(s_dve, chain[0])

                nc.vector.memset(wt1[:, :], 0.0)
                nc.vector.memset(wsc1[:, :], 0.0)
                nc.vector.memset(wbc[:, :], 0.0)
                nc.vector.memset(eps[:, :], EPS).then_inc(s_eps, 1)
                link(nc.vector.memset(wa[:, :], 0.0))
                nc.vector.memset(dstrel[:, NT:], 0.0).then_inc(s_zero, 1)
                dve.wait_ge(s_dq, 16)
                nc.vector.tensor_reduce(dmin[:, :], dq[:, :, :], AX.X, ALU.min)
                link(nc.vector.tensor_reduce(dmax[:, :], dq[:, :, :], AX.X, ALU.max))
                nc.vector.tensor_tensor(spread[:, :], dmax[:, :], dmin[:, :], ALU.subtract).then_inc(s_mm, 1)
                dve.wait_ge(s_x, 16)
                for g in range(NN // 5):
                    sl = slice(5 * g, 5 * g + 5)
                    for t in range(5 * g, 5 * g + 5):
                        ins = nc.vector.bn_stats(stats[:, t, :], x_sb[:, t, :])
                    link(ins)
                    for t in range(5 * g, 5 * g + 5):
                        ins = nc.vector.bn_aggr(meanvar[:, t, :], stats[:, t, :])
                    ins.then_inc(s_stat, 1)
                    dve.wait_ge(s_std, g + 1)
                    link(nc.vector.reciprocal(rstd[:, sl], rstd[:, sl]))
                    nc.vector.scalar_tensor_tensor(nmr[:, sl], meanvar[:, sl, 0], -1.0, rstd[:, sl],
                                                   ALU.mult, ALU.mult).then_inc(s_rstd, 1)
                    if g == 0:
                        dve.wait_ge(s_w, 16 * len(wloads))
                        a, b = S0 ** -0.5, V0 ** -0.5
                        c = (2.0 / 96.0) ** 0.5
                        for ap, k in ((wt1[0:64, :], a), (wt1[64:128, :], b), (wt2[:, :], b), (wsc1[0:64, :], a),
                                      (wsc1[64:128, :], b), (wsc2[:, :], b), (wa[:, :], c), (wbc[0:96, :], c),
                                      (wbc[96:128, :], c * 3.0 ** -0.5)):
                            ins = nc.vector.tensor_scalar_mul(ap, ap, k)
                        ins.then_inc(s_scaled, 1)
                    if g >= 1:
                        for t in range(5 * g - 5, 5 * g):
                            h_columns(t)
                for t in range(NN - 5, NN):
                    h_columns(t)
                dve.wait_ge(s_idx, 48)
                dve.wait_ge(s_mmb, 48)
                link(nc.vector.scalar_tensor_tensor(dstrel[:, 0:NT], dst_sb[:, :], float(WIN), minb[:, :],
                                                    ALU.add, ALU.subtract))
                nc.vector.tensor_scalar_add(base[:, :], base[:, :], -float(WIN))
                link(nc.vector.tensor_reduce(widest[:, :], spreadrow[:, :], AX.X, ALU.max))
                nc.vector.tensor_scalar_add(widest_i[:, :], widest[:, :], 1.0).then_inc(s_spread, 1)
                dve.wait_ge(s_spread, 1)

            @block.tensor
            def _(pe):
                pe.wait_ge(s_ident, 2)
                for t in range(NN + 1):
                    if t < NN:
                        pe.wait_ge(s_h, t + 1)
                        if t >= 2:
                            pe.wait_ge(s_hTsb, t - 1)
                        nc.tensor.transpose(ps[:, t % 2, 0:NTN], h_sb[:, t, 0:128], ident[0:NTN, 0:NTN])
                        nc.tensor.transpose(ps[0:V0, 2 + t % 2, 0:NTN], h_sb[:, t, 128:D],
                                            ident[0:NTN, 0:NTN]).then_inc(s_hT, 1)
                    if t >= 1:
                        u = t - 1
                        if u == 0:
                            pe.wait_ge(s_scaled, 1)
                        pe.wait_ge(s_hTsb, u + 1)
                        if u >= 2:
                            pe.wait_ge(s_tabsb, u - 1)
                        nc.tensor.matmul(ps[0:NTN, 4 + u % 2, 0:128], hT1[:, u, :], wt1[:, 0:128],
                                         start=True, stop=True)
                        nc.tensor.matmul(ps[0:NTN, 4 + u % 2, 128:D], hT2[:, u, :], wt2[:, :],
                                         start=True, stop=True).then_inc(s_tabps, 1)

        p_emb = [sem(f"p_emb{u}") for u in range(SLOTS)]
        p_gath = [sem(f"p_gath{u}") for u in range(SLOTS)]
        p_idx, p_hidps, p_hid, p_w, p_prod, p_S, p_out, p_agg, p_win = (
            sem("p_" + n) for n in ("idx", "hidps", "hid", "w", "prod", "S", "out", "agg", "win"))
        pass_sems = p_emb + p_gath + [p_idx, p_hidps, p_hid, p_w, p_prod, p_S, p_out, p_agg, p_win]

        def hid_ps(u):
            return ps[0:HID, u % 2, :]

        def w_ps(u):
            return ps[:, 2 + 2 * (u % 2):4 + 2 * (u % 2), :].rearrange("p b (j w) -> p (b j) w", j=2)

        def out_ps(u):
            return ps[:, 6 + u % 2, 0:QT * WIN * AC].rearrange("p (j n c) -> p j n c", j=QT, c=AC)

        end = nc.values_load(widest_i[0:1, 0:1], min_val=1, max_val=N,
                             skip_runtime_bounds_check_because="dst lies in [0, N)")

        def passes():
            with nc.Block() as block:
                @block.sync
                def _(sp):
                    def step(i, u):
                        q = i * SLOTS + u
                        if not (isinstance(i, int) and i == 0):
                            sp.wait_ge(p_hidps, q - SLOTS + 1)
                        sp.dma_start(emb[0:NB, u, :],
                                     emb_t[:, bass.ds(q * (QT * TE), QT * TE)]).then_inc(p_emb[u], 16)
                    for u in range(SLOTS):
                        step(0, u)
                    with sp.Fori(1, NI) as i:
                        for u in range(SLOTS):
                            step(i, u)

                @block.gpsimd
                def _(pool):
                    def step(i, u):
                        q = i * SLOTS + u
                        if not (isinstance(i, int) and i == 0):
                            pool.wait_ge(p_prod, q - SLOTS + 1)
                        nc.gpsimd.tensor_copy(idx[:, u, :], src_sb[:, bass.ds(q * QT, QT)]).then_inc(p_idx, 1)
                        pool.wait_ge(p_idx, q + 1)
                        nc.gpsimd.nop(nofuse=True)
                        for j in range(QT):
                            nc.gpsimd.indirect_dma_start(
                                gath[:, u, j, :], None, table,
                                bass.IndirectOffsetOnAxis(ap=idx[:, u, j:j + 1], axis=0)).then_inc(p_gath[u], 16)
                    for u in range(SLOTS):
                        step(0, u)
                    with pool.Fori(1, NI) as i:
                        for u in range(SLOTS):
                            step(i, u)

                @block.scalar
                def _(act):
                    def step(i, u):
                        q = i * SLOTS + u
                        act.wait_ge(p_hidps, q + 1)
                        if not (isinstance(i, int) and q < 2):
                            act.wait_ge(p_w, q - 1)
                        nc.scalar.activation(hid[0:HID, u % 2, :], hid_ps(u), ACT.Silu).then_inc(p_hid, 1)
                    for u in range(SLOTS):
                        step(0, u)
                    with act.Fori(1, NI) as i:
                        for u in range(SLOTS):
                            step(i, u)

                @block.vector
                def _(dve):
                    nc.vector.tensor_scalar_add(dstrel[:, 0:NT], dstrel[:, 0:NT], -float(WIN))
                    nc.vector.tensor_scalar(base[:, :], base[:, :], float(WIN), float(N - 1),
                                            ALU.add, ALU.min).then_inc(p_win, 1)
                    dve.wait_ge(p_win, 1)
                    nc.vector.tensor_scalar_mul(base_i[:, :], base[:, :], float(AC)).then_inc(p_win, 1)
                    dve.wait_ge(p_win, 2)

                    def selector(q, u, j):
                        t = q * QT + j
                        return nc.vector.scalar_tensor_tensor(
                            S[:, u % 2, j, :, :], iota[:, :, :], dstrel[:, bass.ds(t, 1)],
                            sh_sb[:, bass.ds(t, 1), :].broadcast_to([128, WIN, 4]), ALU.is_equal, ALU.mult)

                    def products(i, q, u):
                        dve.wait_ge(p_gath[u], (i + 1) * (16 * QT))
                        dve.wait_ge(p_w, q + 1)
                        w, g = w_ps(u), gath[:, u, :, :]
                        xs = g[:, :, 0:S0].unsqueeze(2).broadcast_to([128, QT, 2, S0])
                        xvec = g[:, :, S0:D].rearrange("p j (c m) -> p j c m", c=NC)
                        pu = P[:, u % 2, :, :]
                        nc.vector.tensor_tensor(pu[:, :, 0:128].rearrange("p j (a m) -> p j a m", a=2),
                                                w[:, :, 0:128].rearrange("p j (a m) -> p j a m", a=2), xs, ALU.mult)
                        for a in range(2):
                            lo = 128 + VD * a
                            wv = w[:, :, 128 + V0 * a:128 + V0 * (a + 1)].unsqueeze(2).broadcast_to([128, QT, NC, V0])
                            ins = nc.vector.tensor_tensor(
                                pu[:, :, lo:lo + VD].rearrange("p j (c m) -> p j c m", c=NC), wv, xvec, ALU.mult)
                        ins.then_inc(p_prod, 1)

                    def add_windows(q, u, more=True):
                        _, cols = nc.values_load_multi_w_load_instructions(
                            base_i[0:1, bass.ds(q * QT, QT)], engines=[mybir.EngineType.DVE], min_val=0,
                            max_val=(N - 1) * AC, skip_runtime_bounds_check_because="base is clamped to [0, N)")
                        dve.wait_ge(p_out, q + 1)
                        for j in range(QT):
                            if more:
                                selector(q + 2, u, j).then_inc(p_S, 1)
                            if not (isinstance(q, int) and q == 0 and j == 0):
                                dve.wait_ge(p_agg, q * QT + j)
                            a = agg[:, bass.ds(cols[j], WIN * AC)]
                            nc.vector.tensor_tensor(a, ps[:, 6 + u % 2, j * WIN * AC:(j + 1) * WIN * AC], a,
                                                    ALU.add).then_inc(p_agg, 1)

                    def step(i, u):
                        q = i * SLOTS + u
                        if isinstance(i, int) and u < 2:
                            for j in range(QT):
                                selector(q, u, j).then_inc(p_S, 1)
                        else:
                            add_windows(q - 2, u)
                        products(i, q, u)
                    for u in range(SLOTS):
                        step(0, u)
                    with dve.Fori(1, NI) as i:
                        for u in range(SLOTS):
                            step(i, u)
                    add_windows(NQ - 2, 0, more=False)
                    add_windows(NQ - 1, 1, more=False)
                    dve.wait_ge(p_agg, NT)

                @block.tensor
                def _(pe):
                    def hidden(i, q, u):
                        pe.wait_ge(p_emb[u], (i + 1) * 16)
                        if not (isinstance(q, int) and q < 2):
                            pe.wait_ge(p_hid, q - 1)
                        nc.tensor.matmul(hid_ps(u), fc1_sb[:, :], emb[:, u, :], start=True,
                                         stop=True).then_inc(p_hidps, 1)

                    def weights(q, u):
                        pe.wait_ge(p_hid, q + 1)
                        if not (isinstance(q, int) and q < 2):
                            pe.wait_ge(p_prod, q - 1)
                        for j in range(QT):
                            ins = nc.tensor.matmul(w_ps(u)[:, j, 0:WN], hid[:, u % 2, j * TE:(j + 1) * TE],
                                                   fc2_sb[:, :], start=True, stop=True)
                        ins.then_inc(p_w, 1)

                    def scatter(q, u):
                        pe.wait_ge(p_prod, q + 1)
                        pe.wait_ge(p_S, q * QT + QT)
                        if not (isinstance(q, int) and q < 2):
                            pe.wait_ge(p_agg, q * QT - QT)
                        for j in range(QT):
                            pj, sj, oj = P[:, u % 2, j, :], S[:, u % 2, j, :, :], out_ps(u)[:, j, :, :]
                            nc.tensor.matmul(oj[:, :, 0:4], pj[:, 0:128], sj, start=True, stop=True)
                            nc.tensor.matmul(oj[0:VD, :, 4], pj[:, 128:128 + VD], sj[:, :, 0], start=True, stop=True)
                            for c in range(NC):
                                lo = 128 + VD + V0 * c
                                ins = nc.tensor.matmul(oj[VD:128, :, 4], pj[:, lo:lo + V0], sj[:, :, 1 + c],
                                                       start=(c == 0), stop=(c == NC - 1), tile_position=(0, VD))
                        ins.then_inc(p_out, 1)

                    def step(i, u):
                        q = i * SLOTS + u
                        first = isinstance(i, int) and i == 0
                        hidden(i, q, u)
                        if not (first and u < 1):
                            weights(q - 1, u - 1)
                        if not (first and u < 2):
                            scatter(q - 2, u)
                    for u in range(SLOTS):
                        step(0, u)
                    with pe.Fori(1, NI) as i:
                        for u in range(SLOTS):
                            step(i, u)
                    weights(NQ - 1, SLOTS - 1)
                    scatter(NQ - 2, 0)
                    scatter(NQ - 1, 1)

            nums = [s.num for s in pass_sems]
            assert max(nums) - min(nums) + 1 == len(nums)
            nc.gpsimd.sem_clear(range(min(nums), max(nums) + 1))
            nc.all_engine_barrier()

        with nc.Fori(0, end, WIN):
            passes()

        e_ps, e_act, e_sum, e_xh, e_gate = (sem("e_" + n) for n in ("ps", "act", "sum", "xh", "gate"))
        e_out = [sem(f"e_out{i}") for i in range(4)]

        def o_ps(t):
            return ps[0:NTN, t % 4, 0:WN]

        with nc.Block() as block:
            @block.tensor
            def _(pe):
                for t in range(NN):
                    if t >= 4:
                        pe.wait_ge(e_gate, t - 3)
                    a = agg_v[:, t * NTN:(t + 1) * NTN, :]
                    o = o_ps(t)
                    nc.tensor.matmul(o, hT1[:, t, :], wsc1[:, :], start=True, stop=False)
                    nc.tensor.matmul(o[:, 160:192], hT2[:, t, :], wsc2[:, :], start=False, stop=False)
                    nc.tensor.matmul(o, a[:, :, 4], wbc[:, :], start=False, stop=False)
                    nc.tensor.matmul(o[:, 0:96], a[:, :, 0], wa[:, 0:96], start=False, stop=False)
                    for c in range(NC):
                        ins = nc.tensor.matmul(o[:, 96 + V0 * c:96 + V0 * (c + 1)], a[:, :, 1 + c],
                                               wa[:, 96:96 + V0], start=False, stop=(c == NC - 1))
                    ins.then_inc(e_ps, 1)

            @block.scalar
            def _(act):
                for t in range(NN):
                    act.wait_ge(e_ps, t + 1)
                    if t >= 4:
                        act.wait_ge(e_sum, t - 3)
                    nc.scalar.activation(act_o[:, t % 4, :], o_ps(t)[:, 0:96], ACT.Silu).then_inc(e_act, 1)

            @block.gpsimd
            def _(pool):
                for g in range(NN // 5):
                    sl = slice(5 * g, 5 * g + 5)
                    nc.gpsimd.tensor_tensor(x_sb[:, sl, 0:S0], x_sb[:, sl, 0:S0], h_sb[:, sl, 0:S0], ALU.add)
                    xo = x_sb[:, sl, S0:D].rearrange("p t (m c) -> p t m c", c=NC)
                    ho = h_sb[:, sl, S0:D].rearrange("p t (c m) -> p t m c", c=NC)
                    nc.gpsimd.tensor_tensor(xo, xo, ho, ALU.add).then_inc(e_xh, 1)

            @block.vector
            def _(dve):
                for t in range(NN):
                    r = res[:, t % 4, :]
                    dve.wait_ge(e_act, t + 1)
                    if t >= 4:
                        dve.wait_ge(e_out[t % 4], 16 * (t // 4))
                    g = act_o[:, t % 4, S0:96].unsqueeze(1).broadcast_to([NTN, NC, V0])
                    v = o_ps(t)[:, 96:192].rearrange("p (c m) -> p c m", c=NC)
                    nc.vector.tensor_tensor(vec(r[:, S0:D]), v, g, ALU.mult).then_inc(e_gate, 1)
                    dve.wait_ge(e_xh, t // 5 + 1)
                    nc.vector.tensor_tensor(r[:, 0:S0], act_o[:, t % 4, 0:S0], x_sb[:, t, 0:S0], ALU.add)
                    dve.wait_ge(e_gate, t + 1)
                    nc.vector.tensor_tensor(r[:, S0:D], r[:, S0:D], x_sb[:, t, S0:D], ALU.add).then_inc(e_sum, 1)

            @block.sync
            def _(sp):
                for t in range(NN):
                    sp.wait_ge(e_sum, t + 1)
                    sp.dma_start(outv[t], res[:, t % 4, :]).then_inc(e_out[t % 4], 16)
                for i in range(4):
                    sp.wait_ge(e_out[i], 16 * len(range(i, NN, 4)))


def kernel(**inputs):
    import numpy as np
    import concourse.bacc as bacc
    from concourse.bass_utils import run_bass_kernel_spmd as run

    a = {k: np.asarray(v) for k, v in inputs.items()}
    pad = EP - E
    src = np.pad(a["src"], (0, pad), mode="edge")
    dst = np.pad(a["dst"], (0, pad), mode="edge")
    sh = np.pad(a["edge_attr_4"], ((0, pad + QT * TE), (0, 0)))
    emb = np.pad(a["edge_attr_8"], ((0, pad), (0, 0)))
    p = "L0_gnn_"
    arrays = {
        "x": a["x"],
        "src_t": src.reshape(NT, TE).T,
        "dst_t": dst.reshape(NT, TE).T,
        "dst_q": dst.reshape(NQ, QT, TE),
        "sh_t": sh.reshape(NT + QT, TE, 4).transpose(1, 0, 2),
        "emb_t": emb.T,
        "w1s": a[p + "W1_s"], "w1v": a[p + "W1_v"],
        "fc1": a[p + "fc_w1"], "fb1": a[p + "fc_b1"][None, :],
        "fc2": a[p + "fc_w2"], "fb2": a[p + "fc_b2"][None, :],
        "w2s": a[p + "W2_s"], "w2v": a[p + "W2_v"],
        "wscs": a[p + "Wsc_s"], "wscv": a[p + "Wsc_v"],
    }
    arrays = {k: np.ascontiguousarray(v) for k, v in arrays.items()}
    nc = bacc.Bacc("TRN2", target_bir_lowering=False, num_devices=1)
    aps = [nc.dram_tensor(k, v.shape, mybir.dt.from_np(v.dtype), kind="ExternalInput").ap() for k, v in arrays.items()]
    o = nc.dram_tensor("out", (N, D), F32, kind="ExternalOutput").ap()
    build(nc, *aps, o)
    r = run(nc, [arrays], core_ids=[0])
    return r.results[0]["out"]
```

```python
from contextlib import ExitStack

import concourse.bass as bass
from concourse import mybir

F32 = mybir.dt.float32
F32R = mybir.dt.float32r
BF16 = mybir.dt.bfloat16
I32 = mybir.dt.int32
ALU = mybir.AluOpType
ACT = mybir.ActivationFunctionType
AX = mybir.AxisListType

N = 3125
E = 53125
D = 160
S0, V0, NC = 64, 32, 3
VD = V0 * NC
NB, HID, WN = 8, 64, 192
TE = 128
QT = 4
NQ = -(-E // (TE * QT))
NT = NQ * QT
EP = NT * TE
SLOTS = 4
NI = NQ // SLOTS
WIN = 16
AC = 4
ES = 3
EW = EP * NB // 128
NTN = 125
NN = N // NTN
EPS = 1e-5
WARM = 11
assert NI * SLOTS == NQ and NN * NTN == N


def build(nc, x, src_t, dst_t, dst_q, sh_t, emb_t, w1s, w1v, fc1, fb1, fc2, fb2, w2s, w2v, wscs, wscv, out):
    ctx = ExitStack()
    with ctx:
        def sb(name, shape, dt=F32):
            return ctx.enter_context(nc.sbuf_tensor(name, shape, dt))

        def sem(name):
            return ctx.enter_context(nc.semaphore(name))

        x_sb = sb("x_sb", [NTN, NN, D])
        h_sb = sb("h_sb", [NTN, NN, D])
        hT1 = sb("hT1", [128, NN, NTN])
        hT2 = sb("hT2", [V0, NN, NTN])
        ident = sb("ident", [128, 128])
        wt1 = sb("wt1", [128, D])
        wt2 = sb("wt2", [V0, V0])
        wsc1 = sb("wsc1", [128, WN])
        wsc2 = sb("wsc2", [V0, V0])
        wo0 = sb("wo0", [128, 160])
        wo1 = sb("wo1", [128, WN])
        wo2 = sb("wo2", [128, V0])
        fc1_in = sb("fc1_in", [NB, HID])
        fc1_hi = sb("fc1_hi", [NB, HID], F32R)
        fc1_lo = sb("fc1_lo", [NB, HID], F32R)
        fc1_sb = sb("fc1_sb", [ES * NB, HID], F32R)
        fb1_sb = sb("fb1_sb", [HID, 1])
        fc2_sb = sb("fc2_sb", [128, WN])
        src_sb = sb("src_sb", [128, NT + QT], I32)
        dstrel = sb("dstrel", [128, NT + QT])
        sh_sb = sb("sh_sb", [128, NT + QT, 4])
        iota = sb("iota", [128, WIN, 4])
        base = sb("base", [1, NT])
        base_i = sb("base_i", [1, NT], I32)
        widest_i = sb("widest_i", [1, 1], I32)
        agg = sb("agg", [128, (N + WIN) * AC])
        ps = ctx.enter_context(nc.psum_tensor("ps", [128, 8, 512], F32))
        table = nc.dram_tensor("table", [N, D], F32, kind="Internal").ap()
        emb_d = nc.dram_tensor("emb_d", [ES, 128, EW], F32, kind="Internal").ap()
        dmin_d = nc.dram_tensor("dmin_d", [NQ, QT], F32, kind="Internal").ap()
        spread_d = nc.dram_tensor("spread_d", [NQ, QT], F32, kind="Internal").ap()

        agg_v = agg[:, 0:N * AC].rearrange("p (n c) -> p n c", c=AC)
        xv = x.rearrange("(t p) d -> p t d", p=NTN)
        outv = out.rearrange("(t p) d -> t p d", p=NTN)

        def vec(ap):
            return ap.rearrange("p (m c) -> p c m", c=NC)

        hid = sb("hid", [128, 2, QT * TE])
        tmp = ctx.enter_context(ExitStack())

        def sbt(name, shape, dt=F32):
            return tmp.enter_context(nc.sbuf_tensor(name, shape, dt))

        stats = sbt("stats", [NTN, NN, 6])
        meanvar = sbt("meanvar", [NTN, NN, 2])
        rstd = sbt("rstd", [NTN, NN])
        nmr = sbt("nmr", [NTN, NN])
        eps = sbt("eps", [NTN, 1])
        tab = sbt("tab", [NTN, 5, D])
        dst_sb = sbt("dst_sb", [128, NT], I32)
        minb = sbt("minb", [128, NT])
        dq = sbt("dq", [NQ, QT, TE], I32)
        dmin = sbt("dmin", [NQ, QT])
        dmax = sbt("dmax", [NQ, QT])
        spread = sbt("spread", [NQ, QT])
        spreadrow = sbt("spreadrow", [1, NT])
        widest = sbt("widest", [1, 1])
        e_in = sbt("e_in", [128, EW])
        e_hi = sbt("e_hi", [128, EW], F32R)
        e_lo = sbt("e_lo", [128, EW], F32R)
        s_x, s_emb0, s_idx, s_dq, s_w, s_zero = (sem("s_" + n) for n in ("x", "emb0", "idx", "dq", "w", "zero"))
        s_eps, s_ident, s_iota, s_ones = (sem("s_" + n) for n in ("eps", "ident", "iota", "ones"))
        s_stat, s_std, s_rstd, s_h, s_hT, s_hTsb = (sem("s_" + n) for n in ("stat", "std", "rstd", "h", "hT", "hTsb"))
        s_tabps, s_tabsb, s_scaled, s_dve = (sem("s_" + n) for n in ("tabps", "tabsb", "scaled", "dve"))
        s_tabw = [sem(f"s_tabw{i}") for i in range(5)]
        s_mm, s_mmout, s_mmb, s_mmrow, s_spread = (sem("s_" + n) for n in ("mm", "mmout", "mmb", "mmrow", "spread"))
        s_ein, s_esplit, s_eout, s_fin, s_fsplit, s_fput = (
            sem("s_" + n) for n in ("ein", "esplit", "eout", "fin", "fsplit", "fput"))
        wloads = [
            (wt1[0:S0, 0:S0], w1s), (wt1[64:96, 64:96], w1v), (wt1[96:128, 96:128], w1v), (wt2[:, :], w1v),
            (wsc1[0:S0, 0:96], wscs), (wsc1[64:96, 96:128], wscv), (wsc1[96:128, 128:160], wscv), (wsc2[:, :], wscv),
            (wo0[0:64, 0:96], w2s[0:S0, :]), (wo0[64:96, 96:128], w2v[S0:96, :]), (wo0[96:128, 128:160], w2v[S0:96, :]),
            (wo1[0:32, 160:192], w2v[S0:96, :]), (wo1[32:64, 0:96], w2s[S0:96, :]), (wo1[64:128, 96:128], w2v[0:S0, :]),
            (wo2[64:128, :], w2v[0:S0, :]),
            (fb1_sb[:, :], fb1), (fc2_sb[0:HID, :], fc2), (fc2_sb[HID:HID + 1, :], fb2),
        ]

        with nc.Block() as block:
            @block.sync
            def _(sp):
                sp.dma_start(x_sb[:, 0:NN, :], xv).then_inc(s_x, 16)
                sp.dma_start(fc1_in[:, :], fc1).then_inc(s_fin, 16)
                sp.dma_start(e_in[:, :], emb_t.rearrange("k (a n) -> (k a) n", n=EW)).then_inc(s_ein, 16)
                sp.wait_ge(s_zero, 1)
                for dst, w in wloads:
                    sp.dma_start(dst, w).then_inc(s_w, 16)
                sp.wait_ge(s_fsplit, 1)
                for part, w in enumerate((fc1_hi, fc1_hi, fc1_lo)):
                    sp.dma_start(fc1_sb[part * NB:(part + 1) * NB, :].bitcast(F32),
                                 w[:, :].bitcast(F32)).then_inc(s_fput, 16)
                sp.wait_ge(s_esplit, 2)
                for part, e in enumerate((e_hi, e_lo, e_hi)):
                    sp.dma_start(emb_d[part], e[:, :].bitcast(F32)).then_inc(s_eout, 16)
                for t in range(NN):
                    sp.wait_ge(s_tabsb, t + 1)
                    sp.dma_start(table[t * NTN:(t + 1) * NTN, :], tab[:, t % 5, :]).then_inc(s_tabw[t % 5], 16)
                for i in range(5):
                    sp.wait_ge(s_tabw[i], 16 * 5)
                sp.wait_ge(s_fput, 16 * ES)
                sp.wait_ge(s_eout, 16 * ES)

            @block.gpsimd
            def _(pool):
                nc.gpsimd.memset(ident[:, :], 0.0).then_inc(s_ident, 1)
                pool.wait_ge(s_ident, 1)
                nc.gpsimd.affine_select(out=ident[:, :], in_=ident[:, :], compare_op=ALU.not_equal, fill=1.0, base=0,
                                        pattern=[[-1, 128]], channel_multiplier=1).then_inc(s_ident, 1)
                nc.gpsimd.iota(iota[:, :, :], pattern=[[1, WIN], [0, 4]], base=0, channel_multiplier=0,
                               allow_small_or_imprecise_dtypes=True).then_inc(s_iota, 1)
                nc.gpsimd.memset(src_sb[:, NT:], 0)
                pool.wait_ge(s_ein, 16)
                nc.gpsimd.tensor_copy(e_hi[:, :], e_in[:, :]).then_inc(s_esplit, 1)
                pool.wait_ge(s_esplit, 1)
                nc.gpsimd.tensor_tensor(e_lo[:, :], e_in[:, :], e_hi[:, :].bitcast(F32), ALU.subtract).then_inc(s_esplit, 1)
                nc.gpsimd.memset(agg[:, :], 0.0).then_inc(s_ones, 1)
                pool.wait_ge(s_iota, 1)
                pool.wait_ge(s_ones, 1)

            @block.scalar
            def _(act):
                def table_rows(t):
                    act.wait_ge(s_tabps, t + 1)
                    if t >= 5:
                        act.wait_ge(s_tabw[t % 5], 16 * (t // 5))
                    nc.scalar.copy(tab[:, t % 5, :], ps[0:NTN, 4 + t % 2, 0:D]).then_inc(s_tabsb, 1)

                act.dma_start(dq[:, :, :], dst_q).then_inc(s_dq, 16)
                act.dma_start(src_sb[:, 0:NT], src_t).then_inc(s_idx, 16)
                act.dma_start(dst_sb[:, :], dst_t).then_inc(s_idx, 16)
                act.dma_start(sh_sb[:, :, :], sh_t).then_inc(s_idx, 16)
                act.wait_ge(s_mm, 1)
                act.dma_start(dmin_d, dmin[:, :]).then_inc(s_mmout, 16)
                act.dma_start(spread_d, spread[:, :]).then_inc(s_mmout, 16)
                act.wait_ge(s_mmout, 32)
                flat = dmin_d.rearrange("q t -> (q t)").unsqueeze(0)
                act.dma_start(minb[:, :], flat.broadcast_to([128, NT])).then_inc(s_mmb, 16)
                act.dma_start(base[:, :], flat).then_inc(s_mmb, 16)
                act.dma_start(spreadrow[:, :], spread_d.rearrange("q t -> (q t)").unsqueeze(0)).then_inc(s_mmb, 16)
                act.wait_ge(s_eps, 1)
                for t in range(NN):
                    if t % 5 == 0:
                        act.wait_ge(s_stat, t // 5 + 1)
                        nc.scalar.activation(rstd[:, t:t + 5], meanvar[:, t:t + 5, 1], ACT.Sqrt,
                                             bias=eps[:, 0:1]).then_inc(s_std, 1)
                        act.wait_ge(s_rstd, t // 5 + 1)
                    r, m = rstd[:, t:t + 1], nmr[:, t:t + 1]
                    nc.scalar.activation(h_sb[:, t, 0:S0], x_sb[:, t, 0:S0], ACT.Relu, bias=m, scale=r)
                    nc.scalar.activation(h_sb[:, t, S0:D].rearrange("p (c m) -> p c m", c=NC), vec(x_sb[:, t, S0:D]),
                                         ACT.Relu, bias=m, scale=r).then_inc(s_h, 1)
                    if t >= 5:
                        table_rows(t - 5)
                for t in range(NN - 5, NN):
                    table_rows(t)

            @block.vector
            def _(dve):
                def h_columns(t):
                    dve.wait_ge(s_hT, t + 1)
                    nc.vector.tensor_copy(hT1[:, t, :], ps[:, t % 2, 0:NTN])
                    nc.vector.tensor_copy(hT2[:, t, :], ps[0:V0, 2 + t % 2, 0:NTN]).then_inc(s_hTsb, 1)

                chain = [0]

                def link(ins):
                    chain[0] += 1
                    ins.then_inc(s_dve, 1)
                    dve.wait_ge(s_dve, chain[0])

                nc.vector.memset(wt1[:, :], 0.0)
                nc.vector.memset(wsc1[:, :], 0.0)
                nc.vector.memset(wo0[:, :], 0.0)
                nc.vector.memset(wo1[:, :], 0.0)
                nc.vector.memset(fc2_sb[:, :], 0.0)
                link(nc.vector.memset(hid[HID:128, :, :], 0.0))
                nc.vector.memset(hid[HID:HID + 1, :, :], 1.0)
                nc.vector.memset(eps[:, :], EPS).then_inc(s_eps, 1)
                nc.vector.memset(wo2[:, :], 0.0)
                nc.vector.memset(dstrel[:, NT:], 0.0).then_inc(s_zero, 1)
                dve.wait_ge(s_dq, 16)
                nc.vector.tensor_reduce(dmin[:, :], dq[:, :, :], AX.X, ALU.min)
                link(nc.vector.tensor_reduce(dmax[:, :], dq[:, :, :], AX.X, ALU.max))
                nc.vector.tensor_tensor(spread[:, :], dmax[:, :], dmin[:, :], ALU.subtract).then_inc(s_mm, 1)
                dve.wait_ge(s_fin, 16)
                link(nc.vector.tensor_copy(fc1_hi[:, :], fc1_in[:, :]))
                nc.vector.tensor_tensor(fc1_lo[:, :], fc1_in[:, :], fc1_hi[:, :].bitcast(F32),
                                        ALU.subtract).then_inc(s_fsplit, 1)
                dve.wait_ge(s_x, 16)
                for g in range(NN // 5):
                    sl = slice(5 * g, 5 * g + 5)
                    for t in range(5 * g, 5 * g + 5):
                        ins = nc.vector.bn_stats(stats[:, t, :], x_sb[:, t, :])
                    link(ins)
                    for t in range(5 * g, 5 * g + 5):
                        ins = nc.vector.bn_aggr(meanvar[:, t, :], stats[:, t, :])
                    ins.then_inc(s_stat, 1)
                    dve.wait_ge(s_std, g + 1)
                    link(nc.vector.reciprocal(rstd[:, sl], rstd[:, sl]))
                    nc.vector.scalar_tensor_tensor(nmr[:, sl], meanvar[:, sl, 0], -1.0, rstd[:, sl],
                                                   ALU.mult, ALU.mult).then_inc(s_rstd, 1)
                    if g == 0:
                        dve.wait_ge(s_w, 16 * len(wloads))
                        a, b = S0 ** -0.5, V0 ** -0.5
                        c = (2.0 / 96.0) ** 0.5
                        for ap, k in ((wt1[0:64, :], a), (wt1[64:128, :], b), (wt2[:, :], b), (wsc1[0:64, :], a),
                                      (wsc1[64:128, :], b), (wsc2[:, :], b), (wo0[:, :], c), (wo1[:, 96:192], c),
                                      (wo1[:, 0:96], c * 3.0 ** -0.5), (wo2[:, :], c)):
                            ins = nc.vector.tensor_scalar_mul(ap, ap, k)
                        ins.then_inc(s_scaled, 1)
                    if g >= 1:
                        for t in range(5 * g - 5, 5 * g):
                            h_columns(t)
                for t in range(NN - 5, NN):
                    h_columns(t)
                dve.wait_ge(s_idx, 48)
                dve.wait_ge(s_mmb, 48)
                link(nc.vector.scalar_tensor_tensor(dstrel[:, 0:NT], dst_sb[:, :], float(WIN), minb[:, :],
                                                    ALU.add, ALU.subtract))
                nc.vector.tensor_scalar_add(base[:, :], base[:, :], -float(WIN))
                link(nc.vector.tensor_reduce(widest[:, :], spreadrow[:, :], AX.X, ALU.max))
                nc.vector.tensor_scalar_add(widest_i[:, :], widest[:, :], 1.0).then_inc(s_spread, 1)
                dve.wait_ge(s_spread, 1)

            @block.tensor
            def _(pe):
                pe.wait_ge(s_ident, 2)
                for t in range(NN + 1):
                    if t < NN:
                        pe.wait_ge(s_h, t + 1)
                        if t >= 2:
                            pe.wait_ge(s_hTsb, t - 1)
                        nc.tensor.transpose(ps[:, t % 2, 0:NTN], h_sb[:, t, 0:128], ident[0:NTN, 0:NTN])
                        nc.tensor.transpose(ps[0:V0, 2 + t % 2, 0:NTN], h_sb[:, t, 128:D],
                                            ident[0:NTN, 0:NTN]).then_inc(s_hT, 1)
                    if t >= 1:
                        u = t - 1
                        if u == 0:
                            pe.wait_ge(s_scaled, 1)
                        pe.wait_ge(s_hTsb, u + 1)
                        if u >= 2:
                            pe.wait_ge(s_tabsb, u - 1)
                        nc.tensor.matmul(ps[0:NTN, 4 + u % 2, 0:128], hT1[:, u, :], wt1[:, 0:128],
                                         start=True, stop=True)
                        nc.tensor.matmul(ps[0:NTN, 4 + u % 2, 128:D], hT2[:, u, :], wt2[:, :],
                                         start=True, stop=True).then_inc(s_tabps, 1)

        tmp.close()
        idx = sb("idx", [128, SLOTS, QT], I32)
        gath = sb("gath", [128, SLOTS, QT, D])
        emb = sb("emb", [ES * NB, SLOTS, QT * TE], F32R)
        P = sb("P", [128, 2, QT, 2 * D])
        S = sb("S", [128, 2, QT, WIN, 4])
        act_o = sb("act_o", [NTN, 4, 96])
        res = sb("res", [NTN, 4, D])
        emb_rows = emb_d.rearrange("s (k a) n -> (s k) (a n)", k=NB)
        p_emb = [sem(f"p_emb{u}") for u in range(SLOTS)]
        p_gath = [sem(f"p_gath{u}") for u in range(SLOTS)]
        p_idx, p_hidps, p_hid, p_w, p_prod, p_S, p_out, p_agg, p_win = (
            sem("p_" + n) for n in ("idx", "hidps", "hid", "w", "prod", "S", "out", "agg", "win"))
        pass_sems = p_emb + p_gath + [p_idx, p_hidps, p_hid, p_w, p_prod, p_S, p_out, p_agg, p_win]

        def hid_ps(u):
            return ps[0:HID, u % 2, :]

        def w_ps(u):
            return ps[:, 2 + 2 * (u % 2):4 + 2 * (u % 2), :].rearrange("p b (j w) -> p (b j) w", j=2)

        def out_ps(u):
            return ps[:, 6 + u % 2, 0:QT * WIN * AC].rearrange("p (j n c) -> p j n c", j=QT, c=AC)

        end = nc.values_load(widest_i[0:1, 0:1], min_val=1, max_val=N,
                             skip_runtime_bounds_check_because="dst lies in [0, N)")

        def passes():
            with nc.Block() as block:
                @block.sync
                def _(sp):
                    def step(i, u):
                        q = i * SLOTS + u
                        if not (isinstance(i, int) and i == 0):
                            sp.wait_ge(p_hidps, q - SLOTS + 1)
                        sp.dma_start(emb[:, u, :].bitcast(F32),
                                     emb_rows[:, bass.ds(q * (QT * TE), QT * TE)]).then_inc(p_emb[u], 16)
                    for u in range(SLOTS):
                        step(0, u)
                    with sp.Fori(1, NI) as i:
                        for u in range(SLOTS):
                            step(i, u)

                @block.gpsimd
                def _(pool):
                    def step(i, u):
                        q = i * SLOTS + u
                        if not (isinstance(i, int) and q < SLOTS - 1):
                            pool.wait_ge(p_prod, q - SLOTS + 2)
                        nc.gpsimd.tensor_copy(idx[:, (u + 1) % SLOTS, :],
                                              src_sb[:, bass.ds(q * QT + QT, QT)]).then_inc(p_idx, 1)
                        pool.wait_ge(p_idx, q + 1)
                        nc.gpsimd.nop(nofuse=True)
                        for j in range(QT):
                            nc.gpsimd.indirect_dma_start(
                                gath[:, u, j, :], None, table,
                                bass.IndirectOffsetOnAxis(ap=idx[:, u, j:j + 1], axis=0)).then_inc(p_gath[u], 16)
                    nc.gpsimd.tensor_copy(idx[:, 0, :], src_sb[:, 0:QT]).then_inc(p_idx, 1)
                    for u in range(SLOTS):
                        step(0, u)
                    with pool.Fori(1, NI) as i:
                        for u in range(SLOTS):
                            step(i, u)

                @block.scalar
                def _(act):
                    def step(i, u):
                        q = i * SLOTS + u
                        act.wait_ge(p_hidps, q + 1)
                        if not (isinstance(i, int) and q < 2):
                            act.wait_ge(p_w, q - 1)
                        nc.scalar.activation(hid[0:HID, u % 2, :], hid_ps(u), ACT.Silu, bias=fb1_sb[:, 0:1]).then_inc(p_hid, 1)
                    for u in range(SLOTS):
                        step(0, u)
                    with act.Fori(1, NI) as i:
                        for u in range(SLOTS):
                            step(i, u)

                @block.vector
                def _(dve):
                    nc.vector.memset(ps[:, 6:8, 0:QT * WIN * AC], 0.0)
                    nc.vector.tensor_scalar_add(dstrel[:, 0:NT], dstrel[:, 0:NT], -float(WIN))
                    nc.vector.tensor_scalar(base[:, :], base[:, :], float(WIN), float(N - 1),
                                            ALU.add, ALU.min).then_inc(p_win, 1)
                    dve.wait_ge(p_win, 1)
                    nc.vector.tensor_scalar_mul(base_i[:, :], base[:, :], float(AC)).then_inc(p_win, 1)
                    dve.wait_ge(p_win, 2)

                    def selector(q, u, j):
                        t = q * QT + j
                        return nc.vector.scalar_tensor_tensor(
                            S[:, u % 2, j, :, :], iota[:, :, :], dstrel[:, bass.ds(t, 1)],
                            sh_sb[:, bass.ds(t, 1), :].broadcast_to([128, WIN, 4]), ALU.is_equal, ALU.mult)

                    def products(i, q, u):
                        dve.wait_ge(p_gath[u], (i + 1) * (16 * QT))
                        dve.wait_ge(p_w, q + 1)
                        w, g = w_ps(u), gath[:, u, :, :]
                        xs = g[:, :, 0:S0].unsqueeze(2).broadcast_to([128, QT, 2, S0])
                        xvec = g[:, :, S0:D].rearrange("p j (c m) -> p j c m", c=NC)
                        pu = P[:, u % 2, :, :]
                        nc.vector.tensor_tensor(pu[:, :, 0:128].rearrange("p j (a m) -> p j a m", a=2),
                                                w[:, :, 0:128].rearrange("p j (a m) -> p j a m", a=2), xs, ALU.mult)
                        for a in range(2):
                            lo = 128 + VD * a
                            wv = w[:, :, 128 + V0 * a:128 + V0 * (a + 1)].unsqueeze(2).broadcast_to([128, QT, NC, V0])
                            ins = nc.vector.tensor_tensor(
                                pu[:, :, lo:lo + VD].rearrange("p j (c m) -> p j c m", c=NC), wv, xvec, ALU.mult)
                        ins.then_inc(p_prod, 1)

                    def add_windows(q, u, more=True):
                        _, cols = nc.values_load_multi_w_load_instructions(
                            base_i[0:1, bass.ds(q * QT, QT)], engines=[mybir.EngineType.DVE], min_val=0,
                            max_val=(N - 1) * AC, skip_runtime_bounds_check_because="base is clamped to [0, N)")
                        dve.wait_ge(p_out, q + 1)
                        for j in range(QT):
                            if more:
                                selector(q + 2, u, j).then_inc(p_S, 1)
                            if not (isinstance(q, int) and q == 0 and j == 0):
                                dve.wait_ge(p_agg, q * QT + j)
                            a = agg[:, bass.ds(cols[j], WIN * AC)]
                            nc.vector.tensor_tensor(a, ps[:, 6 + u % 2, j * WIN * AC:(j + 1) * WIN * AC], a,
                                                    ALU.add).then_inc(p_agg, 1)

                    def step(i, u):
                        q = i * SLOTS + u
                        if isinstance(i, int) and u < 2:
                            for j in range(QT):
                                selector(q, u, j).then_inc(p_S, 1)
                        else:
                            add_windows(q - 2, u)
                        products(i, q, u)
                    for u in range(SLOTS):
                        step(0, u)
                    with dve.Fori(1, NI) as i:
                        for u in range(SLOTS):
                            step(i, u)
                    add_windows(NQ - 2, 0, more=False)
                    add_windows(NQ - 1, 1, more=False)
                    dve.wait_ge(p_agg, NT)

                @block.tensor
                def _(pe):
                    def hidden(i, q, u):
                        pe.wait_ge(p_emb[u], (i + 1) * 16)
                        if not (isinstance(q, int) and q < 2):
                            pe.wait_ge(p_hid, q - 1)
                        nc.tensor.matmul(hid_ps(u), fc1_sb[:, :], emb[:, u, :], start=True,
                                         stop=True).then_inc(p_hidps, 1)

                    def weights(q, u):
                        pe.wait_ge(p_hid, q + 1)
                        if not (isinstance(q, int) and q < 2):
                            pe.wait_ge(p_prod, q - 1)
                        for j in range(QT):
                            ins = nc.tensor.matmul(w_ps(u)[:, j, 0:WN], hid[:, u % 2, j * TE:(j + 1) * TE],
                                                   fc2_sb[:, :], start=True, stop=True)
                        ins.then_inc(p_w, 1)

                    def put(oj, b, c, n, w, sj):
                        nc.tensor.matmul(oj[32 * b:32 * b + 32, :, c:c + n], w, sj[:, :, c:c + n],
                                         start=True, stop=True, tile_position=(0, 32 * b))

                    def scatter(q, u):
                        pe.wait_ge(p_prod, q + 1)
                        pe.wait_ge(p_S, q * QT + QT)
                        if not (isinstance(q, int) and q < 2):
                            pe.wait_ge(p_agg, q * QT - QT)
                        for j in range(QT):
                            pj, sj, oj = P[:, u % 2, j, :], S[:, u % 2, j, :, :], out_ps(u)[:, j, :, :]
                            vs, vv = pj[:, 128:128 + VD], pj[:, 128 + VD:128 + 2 * VD]
                            for b in range(2):
                                put(oj, b, 0, 1, pj[:, 32 * b:32 * b + 32], sj)
                            for b in range(2, 4):
                                put(oj, b, 1, 3, pj[:, 32 * b:32 * b + 32], sj)
                            for b in (2, 3):
                                put(oj, b, 0, 1, vs[:, 32 * (b - 2):32 * (b - 1)], sj)
                            nc.tensor.matmul(oj[0:32, :, 1], vs[:, 64:96], sj[:, :, 0], start=True, stop=True,
                                             tile_position=(0, 0))
                            for c in range(NC):
                                ins = nc.tensor.matmul(oj[32:64, :, 1], vv[:, V0 * c:V0 * (c + 1)], sj[:, :, 1 + c],
                                                       start=(c == 0), stop=(c == NC - 1), tile_position=(0, 32))
                        ins.then_inc(p_out, 1)

                    def step(i, u):
                        q = i * SLOTS + u
                        first = isinstance(i, int) and i == 0
                        hidden(i, q, u)
                        if not (first and u < 1):
                            weights(q - 1, u - 1)
                        if not (first and u < 2):
                            scatter(q - 2, u)
                    for _ in range(WARM):
                        nc.tensor.matmul(w_ps(0)[:, 0, 0:WN], fc2_sb[:, 0:128], fc2_sb[:, :], start=True, stop=True)
                    for u in range(SLOTS):
                        step(0, u)
                    with pe.Fori(1, NI) as i:
                        for u in range(SLOTS):
                            step(i, u)
                    weights(NQ - 1, SLOTS - 1)
                    scatter(NQ - 2, 0)
                    scatter(NQ - 1, 1)

            nums = [s.num for s in pass_sems]
            assert max(nums) - min(nums) + 1 == len(nums)
            nc.gpsimd.sem_clear(range(min(nums), max(nums) + 1))
            nc.all_engine_barrier()

        with nc.Fori(0, end, WIN):
            passes()

        e_ps, e_act, e_sum, e_xh, e_gate = (sem("e_" + n) for n in ("ps", "act", "sum", "xh", "gate"))
        e_out = [sem(f"e_out{i}") for i in range(4)]

        def o_ps(t):
            return ps[0:NTN, t % 4, 0:WN]

        with nc.Block() as block:
            @block.tensor
            def _(pe):
                for t in range(NN):
                    if t >= 4:
                        pe.wait_ge(e_gate, t - 3)
                    a = agg_v[:, t * NTN:(t + 1) * NTN, :]
                    o = o_ps(t)
                    nc.tensor.matmul(o, hT1[:, t, :], wsc1[:, :], start=True, stop=False)
                    nc.tensor.matmul(o[:, 160:192], hT2[:, t, :], wsc2[:, :], start=False, stop=False)
                    nc.tensor.matmul(o, a[:, :, 1], wo1[:, :], start=False, stop=False)
                    nc.tensor.matmul(o[:, 0:160], a[:, :, 0], wo0[:, :], start=False, stop=False)
                    nc.tensor.matmul(o[:, 128:160], a[:, :, 2], wo2[:, :], start=False, stop=False)
                    ins = nc.tensor.matmul(o[:, 160:192], a[:, :, 3], wo2[:, :], start=False, stop=True)
                    ins.then_inc(e_ps, 1)

            @block.scalar
            def _(act):
                for t in range(NN):
                    act.wait_ge(e_ps, t + 1)
                    if t >= 4:
                        act.wait_ge(e_sum, t - 3)
                    nc.scalar.activation(act_o[:, t % 4, :], o_ps(t)[:, 0:96], ACT.Silu).then_inc(e_act, 1)

            @block.gpsimd
            def _(pool):
                for g in range(NN // 5):
                    sl = slice(5 * g, 5 * g + 5)
                    nc.gpsimd.tensor_tensor(x_sb[:, sl, 0:S0], x_sb[:, sl, 0:S0], h_sb[:, sl, 0:S0], ALU.add)
                    xo = x_sb[:, sl, S0:D].rearrange("p t (m c) -> p t m c", c=NC)
                    ho = h_sb[:, sl, S0:D].rearrange("p t (c m) -> p t m c", c=NC)
                    nc.gpsimd.tensor_tensor(xo, xo, ho, ALU.add).then_inc(e_xh, 1)

            @block.vector
            def _(dve):
                for t in range(NN):
                    r = res[:, t % 4, :]
                    dve.wait_ge(e_act, t + 1)
                    if t >= 4:
                        dve.wait_ge(e_out[t % 4], 16 * (t // 4))
                    g = act_o[:, t % 4, S0:96].unsqueeze(1).broadcast_to([NTN, NC, V0])
                    v = o_ps(t)[:, 96:192].rearrange("p (c m) -> p c m", c=NC)
                    nc.vector.tensor_tensor(vec(r[:, S0:D]), v, g, ALU.mult).then_inc(e_gate, 1)
                    dve.wait_ge(e_xh, t // 5 + 1)
                    nc.vector.tensor_tensor(r[:, 0:S0], act_o[:, t % 4, 0:S0], x_sb[:, t, 0:S0], ALU.add)
                    dve.wait_ge(e_gate, t + 1)
                    nc.vector.tensor_tensor(r[:, S0:D], r[:, S0:D], x_sb[:, t, S0:D], ALU.add).then_inc(e_sum, 1)

            @block.sync
            def _(sp):
                for t in range(NN):
                    sp.wait_ge(e_sum, t + 1)
                    sp.dma_start(outv[t], res[:, t % 4, :]).then_inc(e_out[t % 4], 16)
                for i in range(4):
                    sp.wait_ge(e_out[i], 16 * len(range(i, NN, 4)))


def kernel(**inputs):
    import numpy as np
    import concourse.bacc as bacc
    from concourse.bass_utils import run_bass_kernel_spmd as run

    a = {k: np.asarray(v) for k, v in inputs.items()}
    pad = EP - E
    src = np.pad(a["src"], (0, pad), mode="edge")
    dst = np.pad(a["dst"], (0, pad), mode="edge")
    sh = np.pad(a["edge_attr_4"], ((0, pad + QT * TE), (0, 0)))
    emb = np.pad(a["edge_attr_8"], ((0, pad), (0, 0)))
    p = "L0_gnn_"
    arrays = {
        "x": a["x"],
        "src_t": src.reshape(NT, TE).T,
        "dst_t": dst.reshape(NT, TE).T,
        "dst_q": dst.reshape(NQ, QT, TE),
        "sh_t": sh.reshape(NT + QT, TE, 4).transpose(1, 0, 2),
        "emb_t": emb.T,
        "w1s": a[p + "W1_s"], "w1v": a[p + "W1_v"],
        "fc1": a[p + "fc_w1"], "fb1": a[p + "fc_b1"][:, None],
        "fc2": a[p + "fc_w2"], "fb2": a[p + "fc_b2"][None, :],
        "w2s": a[p + "W2_s"], "w2v": a[p + "W2_v"],
        "wscs": a[p + "Wsc_s"], "wscv": a[p + "Wsc_v"],
    }
    arrays = {k: np.ascontiguousarray(v) for k, v in arrays.items()}
    nc = bacc.Bacc("TRN2", target_bir_lowering=False, num_devices=1)
    aps = [nc.dram_tensor(k, v.shape, mybir.dt.from_np(v.dtype), kind="ExternalInput").ap() for k, v in arrays.items()]
    o = nc.dram_tensor("out", (N, D), F32, kind="ExternalOutput").ap()
    build(nc, *aps, o)
    r = run(nc, [arrays], core_ids=[0])
    return r.results[0]["out"]
```

```python
from contextlib import ExitStack

import concourse.bass as bass
from concourse import mybir

F32 = mybir.dt.float32
I32 = mybir.dt.int32
ALU = mybir.AluOpType
ACT = mybir.ActivationFunctionType
AX = mybir.AxisListType

N = 3125
E = 53125
D = 160
S0, V0, NC = 64, 32, 3
VD = V0 * NC
NB, HID, WN = 8, 64, 192
TE = 128
QT = 4
NQ = -(-E // (TE * QT))
NT = NQ * QT
EP = NT * TE
SLOTS = 4
NI = NQ // SLOTS
RES = 8
WIN = 16
AC = 3
NTN = 125
NN = N // NTN
G = 5
NG = NN // G
PW = 96 + D + VD
LAG = 4
EPS = 1e-5
WARM_NODES = 20
WARM = 14
WARM_LAST, WARM_END = 8, 4
assert NI * SLOTS == NQ and NN * NTN == N and NG * G == NN


def build(nc, x, src_t, dst_t, dst_q, sh_t, emb_t, w1s, w1v, fc1, fb1, fc2, fb2, w2s, w2v, wscs, wscv, out):
    ctx = ExitStack()
    with ctx:
        def sb(name, shape, dt=F32):
            return ctx.enter_context(nc.sbuf_tensor(name, shape, dt))

        def sem(name):
            return ctx.enter_context(nc.semaphore(name))

        x_sb = sb("x_sb", [NTN, NN, D])
        h_sb = sb("h_sb", [NTN, NN, D])
        prod_flat = sb("prod_flat", [NTN, NN * PW + 2 * (96 + D) - PW])
        prod = prod_flat[:, 0:NN * PW].rearrange("p (t w) -> p t w", w=PW)
        wo0 = sb("wo0", [128, 96 + V0])
        wo1 = sb("wo1", [128, 2 * V0])
        wo2 = sb("wo2", [128, 2 * V0])
        fc1_sb = sb("fc1_sb", [128, HID])
        emb = sb("emb", [128, SLOTS, QT * TE])
        fb1_sb = sb("fb1_sb", [HID, 1])
        fc2_sb = sb("fc2_sb", [128, WN])
        src_sb = sb("src_sb", [128, NT + (SLOTS - 1) * QT], I32)
        dstrel = sb("dstrel", [128, NT + QT])
        sh_sb = sb("sh_sb", [128, NT + QT, 4])
        iota = sb("iota", [128, WIN, 4])
        base = sb("base", [1, NT])
        base_i = sb("base_i", [1, NT], I32)
        widest_i = sb("widest_i", [1, 1], I32)
        agg = sb("agg", [128, (N + WIN) * AC])
        ps = ctx.enter_context(nc.psum_tensor("ps", [128, 8, 512], F32))
        table = nc.dram_tensor("table", [N, D], F32, kind="Internal").ap()
        dmin_d = nc.dram_tensor("dmin_d", [NQ, QT], F32, kind="Internal").ap()
        spread_d = nc.dram_tensor("spread_d", [NQ, QT], F32, kind="Internal").ap()

        agg_v = agg[:, 0:N * AC].rearrange("p (n c) -> p n c", c=AC)
        xv = x.rearrange("(t p) d -> p t d", p=NTN)
        tablev = table.rearrange("(t p) d -> p t d", p=NTN)
        outv = out.rearrange("(t p) d -> t p d", p=NTN)

        def vec(ap):
            return ap.rearrange("p (m c) -> p c m", c=NC)

        hid = sb("hid", [128, 2, QT * TE])
        tmp = ctx.enter_context(ExitStack())

        def sbt(name, shape, dt=F32):
            return tmp.enter_context(nc.sbuf_tensor(name, shape, dt))

        ident = sbt("ident", [128, 128])
        stats = sbt("stats", [NTN, NN, 6])
        meanvar = sbt("meanvar", [NTN, NN, 2])
        rstd = sbt("rstd", [NTN, NN])
        nmr = sbt("nmr", [NTN, NN])
        eps = sbt("eps", [NTN, 1])
        root = sbt("root", [NTN, 1])
        hT = sbt("hT", [VD, 4, 2, NTN])
        w_s = sbt("w_s", [VD, 96 + S0])
        w_v = sbt("w_v", [VD, 2, NC, V0])
        w_v_in = sbt("w_v_in", [VD, 2, V0])
        own_c = sbt("own_c", [VD, NC])
        dst_sb = sbt("dst_sb", [128, NT], I32)
        minb = sbt("minb", [128, NT])
        dq = sbt("dq", [NQ, QT, TE], I32)
        dmin = sbt("dmin", [NQ, QT])
        dmax = sbt("dmax", [NQ, QT])
        spread = sbt("spread", [NQ, QT])
        spreadrow = sbt("spreadrow", [1, NT])
        widest = sbt("widest", [1, 1])
        s_x = [sem(f"s_x{g}") for g in range(NG)]
        s_idx, s_dq, s_wn, s_wo, s_oz = (sem("s_" + n) for n in ("idx", "dq", "wn", "wo", "oz"))
        s_eps, s_ident, s_iota, s_agg = (sem("s_" + n) for n in ("eps", "ident", "iota", "agg"))
        s_stat, s_std, s_rstd, s_h, s_hT, s_hTsb = (sem("s_" + n) for n in ("stat", "std", "rstd", "h", "hT", "hTsb"))
        s_tstat = sem("s_tstat")
        s_prod, s_sb, s_tabw, s_scaled, s_dve = (
            sem("s_" + n) for n in ("prod", "sb", "tabw", "scaled", "dve"))
        s_mm, s_mmout, s_mmb, s_spread = (sem("s_" + n) for n in ("mm", "mmout", "mmb", "spread"))
        node_loads = [
            (w_s[0:S0, 0:96], wscs), (w_s[0:S0, 96:160], w1s),
            (w_v_in[:, 0, :], w1v.unsqueeze(1).broadcast_to([V0, NC, V0])),
            (w_v_in[:, 1, :], wscv.unsqueeze(1).broadcast_to([V0, NC, V0])),
        ]
        other_loads = [
            (fc1_sb[0:NB, :], fc1), (fb1_sb[:, :], fb1), (fc2_sb[0:HID, :], fc2), (fc2_sb[HID:HID + 1, :], fb2),
            (wo0[0:96, 0:96], w2s), (wo0[96:128, 96:128], w2v[S0:96, :]),
            (wo1[0:64, 0:V0], w2v[0:S0, :]), (wo1[64:128, V0:2 * V0], w2v[0:S0, :]),
            (wo2[0:64, V0:2 * V0], w2v[0:S0, :]), (wo2[64:96, 0:V0], w2v[S0:96, :]),
            (wo2[96:128, V0:2 * V0], w2v[S0:96, :]),
        ]

        def hT_ps(t):
            return ps[0:VD, t % 4, 0:2 * NTN].rearrange("p (a n) -> p a n", a=2)

        def prod_ps(t):
            return ps[0:NTN, 4 + t % 4, 0:PW]

        with nc.Block() as block:
            @block.sync
            def _(sp):
                for g in range(NG):
                    sp.dma_start(x_sb[:, g * G:g * G + G, :], xv[:, g * G:g * G + G, :]).then_inc(s_x[g], 16)
                    if g == 0:
                        for dst, w in node_loads:
                            sp.dma_start(dst, w).then_inc(s_wn, 16)
                sp.dma_start(dq[:, :, :], dst_q).then_inc(s_dq, 16)
                sp.dma_start(dst_sb[:, :], dst_t).then_inc(s_idx, 16)
                sp.dma_start(src_sb[:, 0:NT], src_t).then_inc(s_idx, 16)
                sp.dma_start(sh_sb[:, :, :], sh_t).then_inc(s_idx, 16)
                sp.wait_ge(s_oz, 1)
                for dst, w in other_loads:
                    sp.dma_start(dst, w).then_inc(s_wo, 16)
                stores = [(g * G, g * G + G) for g in range(NG - 1)] + [(NN - G, NN - 2), (NN - 2, NN)]
                for t0, t1 in stores:
                    sp.wait_ge(s_sb, t1)
                    sp.dma_start(tablev[:, t0:t1, :], prod[:, t0:t1, 96:96 + D]).then_inc(s_tabw, 16)
                sp.wait_ge(s_tabw, 16 * len(stores))

            @block.gpsimd
            def _(pool):
                nc.gpsimd.memset(ident[:, :], 0.0).then_inc(s_ident, 1)
                pool.wait_ge(s_ident, 1)
                nc.gpsimd.affine_select(out=ident[:, :], in_=ident[:, :], compare_op=ALU.not_equal, fill=1.0, base=0,
                                        pattern=[[-1, 128]], channel_multiplier=1).then_inc(s_ident, 1)
                nc.gpsimd.memset(fc1_sb[:, :], 0.0)
                nc.gpsimd.memset(fc2_sb[:, :], 0.0)
                nc.gpsimd.memset(wo0[:, :], 0.0)
                nc.gpsimd.memset(wo1[:, :], 0.0)
                nc.gpsimd.memset(wo2[:, :], 0.0).then_inc(s_oz, 1)
                nc.gpsimd.memset(src_sb[:, NT:], 0)
                nc.gpsimd.memset(dstrel[:, NT:], 0.0)
                nc.gpsimd.iota(iota[:, :, :], pattern=[[1, WIN], [0, 4]], base=0, channel_multiplier=0,
                               allow_small_or_imprecise_dtypes=True).then_inc(s_iota, 1)
                nc.gpsimd.memset(hid[:, :, :], 0.0).then_inc(s_agg, 1)
                nc.gpsimd.memset(emb[:, :, :], 0.0).then_inc(s_agg, 1)
                nc.gpsimd.memset(agg[:, :], 0.0).then_inc(s_agg, 1)
                pool.wait_ge(s_agg, 3)
                nc.gpsimd.memset(hid[HID:HID + 1, :, :], 1.0).then_inc(s_agg, 1)
                pool.wait_ge(s_mm, 1)
                nc.gpsimd.dma_start(dmin_d, dmin[:, :]).then_inc(s_mmout, 16)
                nc.gpsimd.dma_start(spread_d, spread[:, :]).then_inc(s_mmout, 16)
                pool.wait_ge(s_mmout, 32)
                flat = dmin_d.rearrange("q t -> (q t)").unsqueeze(0)
                nc.gpsimd.dma_start(minb[:, :], flat.broadcast_to([128, NT])).then_inc(s_mmb, 16)
                nc.gpsimd.dma_start(base[:, :], flat).then_inc(s_mmb, 16)
                nc.gpsimd.dma_start(spreadrow[:, :], spread_d.rearrange("q t -> (q t)").unsqueeze(0)).then_inc(
                    s_mmb, 16)
                pool.wait_ge(s_iota, 1)
                pool.wait_ge(s_agg, 4)

            @block.scalar
            def _(act):
                def std(g):
                    act.wait_ge(s_stat, g + 1)
                    sl = slice(g * G, g * G + G)
                    nc.scalar.activation(rstd[:, sl], meanvar[:, sl, 1], ACT.Sqrt, bias=eps[:, 0:1]).then_inc(s_std, 1)

                def products(t):
                    act.wait_ge(s_prod, t + 1)
                    nc.scalar.copy(prod[:, t, :], prod_ps(t)).then_inc(s_sb, 1)

                act.wait_ge(s_eps, 1)
                nc.scalar.activation(root[:, :], eps[:, :], ACT.Sqrt)
                std(0)
                for g in range(NG):
                    act.wait_ge(s_rstd, g + 1)
                    for t in range(g * G, g * G + G):
                        nc.scalar.activation(h_sb[:, t, :], x_sb[:, t, :], ACT.Relu, bias=nmr[:, t:t + 1],
                                             scale=rstd[:, t:t + 1]).then_inc(s_h, 1)
                        if t % G == 1 and g + 1 < NG:
                            std(g + 1)
                        if t >= LAG:
                            products(t - LAG)
                for t in range(NN - LAG, NN):
                    products(t)

            @block.vector
            def _(dve):
                chain = [0]

                def link(ins):
                    chain[0] += 1
                    ins.then_inc(s_dve, 1)
                    dve.wait_ge(s_dve, chain[0])

                def tile_stats(t):
                    if t % G == 0:
                        dve.wait_ge(s_x[t // G], 16)
                    nc.vector.bn_stats(stats[:, t, :], x_sb[:, t, :]).then_inc(s_tstat, 1)

                def mean_and_variance(g):
                    dve.wait_ge(s_tstat, g * G + G)
                    for t in range(g * G, g * G + G):
                        ins = nc.vector.bn_aggr(meanvar[:, t, :], stats[:, t, :])
                    ins.then_inc(s_stat, 1)

                def scale_and_bias(g):
                    sl = slice(g * G, g * G + G)
                    dve.wait_ge(s_std, g + 1)
                    link(nc.vector.reciprocal(rstd[:, sl], rstd[:, sl]))
                    nc.vector.scalar_tensor_tensor(nmr[:, sl], meanvar[:, sl, 0], -1.0, rstd[:, sl],
                                                   ALU.mult, ALU.mult).then_inc(s_rstd, 1)

                def h_columns(t):
                    dve.wait_ge(s_hT, t + 1)
                    if t >= 4:
                        dve.wait_ge(s_prod, t - 3)
                    nc.vector.tensor_copy(hT[:, t % 4, :, :], hT_ps(t)).then_inc(s_hTsb, 1)

                def minima():
                    dve.wait_ge(s_dq, 16)
                    nc.vector.tensor_reduce(dmin[:, :], dq[:, :, :], AX.X, ALU.min)
                    link(nc.vector.tensor_reduce(dmax[:, :], dq[:, :, :], AX.X, ALU.max))
                    nc.vector.tensor_tensor(spread[:, :], dmax[:, :], dmin[:, :], ALU.subtract).then_inc(s_mm, 1)

                def output_weights():
                    dve.wait_ge(s_wo, 16 * len(other_loads))
                    for ap, k in ((wo0[0:64, :], c), (wo0[64:96, :], c * 3.0 ** -0.5), (wo0[96:128, :], c), (wo1[:, :], c),
                                  (wo2[:, :], c)):
                        nc.vector.tensor_scalar_mul(ap, ap, k)

                def windows():
                    dve.wait_ge(s_idx, 48)
                    dve.wait_ge(s_mmb, 48)
                    link(nc.vector.scalar_tensor_tensor(dstrel[:, 0:NT], dst_sb[:, :], float(WIN), minb[:, :],
                                                        ALU.add, ALU.subtract))
                    nc.vector.tensor_scalar_add(base[:, :], base[:, :], -float(WIN))
                    link(nc.vector.tensor_reduce(widest[:, :], spreadrow[:, :], AX.X, ALU.max))
                    nc.vector.tensor_scalar_add(widest_i[:, :], widest[:, :], 1.0).then_inc(s_spread, 1)
                    dve.wait_ge(s_spread, 1)

                nc.vector.memset(eps[:, :], EPS).then_inc(s_eps, 1)
                nc.vector.memset(ps[64:96, 0:4, 0:2 * NTN], 0.0).then_inc(s_eps, 1)
                nc.vector.memset(w_s[S0:VD, :], 0.0)
                a, b, c = S0 ** -0.5, V0 ** -0.5, (2.0 / 96.0) ** 0.5
                dve.wait_ge(s_ident, 2)
                link(nc.vector.tensor_reduce(own_c[:, :], ident[0:VD, 0:VD].rearrange("p (m c) -> p c m", c=NC),
                                             AX.X, ALU.add))
                link(nc.vector.tensor_scalar_mul(own_c[:, :], own_c[:, :], b))
                for t in range(G):
                    tile_stats(t)
                mean_and_variance(0)
                scale_and_bias(0)
                dve.wait_ge(s_wn, 16 * len(node_loads))
                nc.vector.tensor_scalar_mul(w_s[0:S0, :], w_s[0:S0, :], a)
                for k in range(2):
                    ins = nc.vector.tensor_tensor(
                        w_v[:, k, :, :], w_v_in[:, k, :].unsqueeze(1).broadcast_to([VD, NC, V0]),
                        own_c[:, :].unsqueeze(2).broadcast_to([VD, NC, V0]), ALU.mult)
                ins.then_inc(s_scaled, 1)
                for t in range(G, 2 * G):
                    tile_stats(t)
                mean_and_variance(1)
                for g in range(NG):
                    for k in range(G):
                        t = g * G + k
                        h_columns(t)
                        if t == 3 * G:
                            minima()
                        if g + 2 < NG:
                            tile_stats(t + 2 * G)
                        if k == 2 and g + 1 < NG:
                            scale_and_bias(g + 1)
                    if g + 2 < NG:
                        mean_and_variance(g + 2)
                output_weights()
                windows()

            @block.tensor
            def _(pe):
                pe.wait_ge(s_ident, 2)
                for _ in range(WARM_NODES):
                    nc.tensor.matmul(ps[:, 7, 0:128], ident[:, :], ident[:, :], start=True, stop=True)
                pe.wait_ge(s_eps, 2)
                for t in range(NN + 2):
                    if t < NN:
                        pe.wait_ge(s_h, t + 1)
                        if t >= 4:
                            pe.wait_ge(s_hTsb, t - 3)
                        nc.tensor.transpose(hT_ps(t)[0:S0, 0, :], h_sb[:, t, 0:S0], ident[0:NTN, 0:NTN])
                        nc.tensor.transpose(hT_ps(t)[:, 1, :], h_sb[:, t, S0:D],
                                            ident[0:NTN, 0:NTN]).then_inc(s_hT, 1)
                    if t >= 2:
                        u = t - 2
                        if u == 0:
                            pe.wait_ge(s_scaled, 1)
                        pe.wait_ge(s_hTsb, u + 1)
                        if u >= 4:
                            pe.wait_ge(s_sb, u - 3)
                        nc.tensor.matmul(prod_ps(u)[:, 0:160], hT[:, u % 4, 0, :], w_s[:, :],
                                         start=True, stop=True)
                        nc.tensor.matmul(prod_ps(u)[:, 160:352], hT[:, u % 4, 1, :], w_v.rearrange("p a c k -> p (a c k)"),
                                         start=True, stop=True).then_inc(s_prod, 1)

        tmp.close()
        idx = sb("idx", [128, SLOTS, QT], I32)
        gath = sb("gath", [128, SLOTS, QT, D])
        P = sb("P", [128, 2, QT, 2 * D])
        S = sb("S", [128, 2, QT, WIN, 4])
        total = sb("total", [NTN, 4, WN])
        gates = sb("gates", [NTN, 4, V0])
        res = sb("res", [NTN, RES, D])
        p_emb = [sem(f"p_emb{u}") for u in range(SLOTS)]
        p_gath = [sem(f"p_gath{u}") for u in range(SLOTS)]
        p_idx0, p_idx, p_hidps, p_hid, p_w, p_prod, p_S, p_out, p_agg, p_win = (
            sem("p_" + n) for n in ("idx0", "idx", "hidps", "hid", "w", "prod", "S", "out", "agg", "win"))
        pass_sems = p_emb + p_gath + [p_idx0, p_idx, p_hidps, p_hid, p_w, p_prod, p_S, p_out, p_agg, p_win]

        def hid_ps(u):
            return ps[0:HID, u % 2, :]

        def w_ps(u):
            return ps[:, 2 + 2 * (u % 2):4 + 2 * (u % 2), :].rearrange("p b (j w) -> p (b j) w", j=2)

        def out_ps(u):
            return ps[:, 6 + u % 2, 0:QT * WIN * AC].rearrange("p (j n c) -> p j n c", j=QT, c=AC)

        end = nc.values_load(widest_i[0:1, 0:1], min_val=1, max_val=N,
                             skip_runtime_bounds_check_because="dst lies in [0, N)")

        def passes():
            with nc.Block() as block:
                @block.sync
                def _(sp):
                    def step(i, u):
                        q = i * SLOTS + u
                        if not (isinstance(i, int) and i == 0):
                            sp.wait_ge(p_hidps, q - SLOTS + 1)
                        sp.dma_start(emb[0:NB, u, :],
                                     emb_t[:, bass.ds(q * (QT * TE), QT * TE)]).then_inc(p_emb[u], 16)
                    for u in range(SLOTS):
                        step(0, u)
                    with sp.Fori(1, NI) as i:
                        for u in range(SLOTS):
                            step(i, u)

                @block.gpsimd
                def _(pool):
                    def step(i, u):
                        q = i * SLOTS + u
                        if not (isinstance(i, int) and i == 0):
                            pool.wait_ge(p_prod, q - SLOTS + 1)
                        if isinstance(q, int) and q < SLOTS - 1:
                            pool.wait_ge(p_idx0, 1)
                        else:
                            pool.wait_ge(p_idx, q - SLOTS + 2)
                        nc.gpsimd.nop(nofuse=True)
                        for j in range(QT):
                            nc.gpsimd.indirect_dma_start(
                                gath[:, u, j, :], None, table,
                                bass.IndirectOffsetOnAxis(ap=idx[:, u, j:j + 1], axis=0)).then_inc(p_gath[u], 16)
                    nc.gpsimd.tensor_copy(idx[:, 0:SLOTS - 1, :], src_sb[:, 0:(SLOTS - 1) * QT].rearrange(
                        "p (q j) -> p q j", j=QT)).then_inc(p_idx0, 1)
                    for u in range(SLOTS):
                        step(0, u)
                    with pool.Fori(1, NI) as i:
                        for u in range(SLOTS):
                            step(i, u)
                    for u in range(SLOTS):
                        pool.wait_ge(p_gath[u], NI * (16 * QT))

                @block.scalar
                def _(act):
                    def indices(q, u):
                        nc.scalar.copy(idx[:, u, :], src_sb[:, bass.ds(q * QT, QT)]).then_inc(p_idx, 1)

                    def step(i, u):
                        q = i * SLOTS + u
                        act.wait_ge(p_hidps, q + 1)
                        if not (isinstance(i, int) and q < 2):
                            act.wait_ge(p_w, q - 1)
                        nc.scalar.activation(hid[0:HID, u % 2, :], hid_ps(u), ACT.Silu, bias=fb1_sb[:, 0:1]).then_inc(p_hid, 1)
                        if not (isinstance(i, int) and q < 1):
                            act.wait_ge(p_prod, q)
                        indices(q + SLOTS - 1, (u + SLOTS - 1) % SLOTS)
                    for u in range(SLOTS):
                        step(0, u)
                    with act.Fori(1, NI) as i:
                        for u in range(SLOTS):
                            step(i, u)

                @block.vector
                def _(dve):
                    nc.vector.tensor_scalar_add(dstrel[:, 0:NT], dstrel[:, 0:NT], -float(WIN))
                    nc.vector.tensor_scalar(base[:, :], base[:, :], float(WIN), float(N - 1),
                                            ALU.add, ALU.min).then_inc(p_win, 1)
                    dve.wait_ge(p_win, 1)
                    nc.vector.tensor_scalar_mul(base_i[:, :], base[:, :], float(AC)).then_inc(p_win, 1)
                    dve.wait_ge(p_win, 2)

                    def selector(q, u, j):
                        t = q * QT + j
                        return nc.vector.scalar_tensor_tensor(
                            S[:, u % 2, j, :, :], iota[:, :, :], dstrel[:, bass.ds(t, 1)],
                            sh_sb[:, bass.ds(t, 1), :].broadcast_to([128, WIN, 4]), ALU.is_equal, ALU.mult)

                    def products(i, q, u):
                        dve.wait_ge(p_gath[u], (i + 1) * (16 * QT))
                        dve.wait_ge(p_w, q + 1)
                        w, g = w_ps(u), gath[:, u, :, :]
                        xs = g[:, :, 0:S0].unsqueeze(2).broadcast_to([128, QT, 2, S0])
                        xvec = g[:, :, S0:D].rearrange("p j (c m) -> p j c m", c=NC)
                        pu = P[:, u % 2, :, :]
                        nc.vector.tensor_tensor(pu[:, :, 0:128].rearrange("p j (a m) -> p j a m", a=2),
                                                w[:, :, 0:128].rearrange("p j (a m) -> p j a m", a=2), xs, ALU.mult)
                        for a in range(2):
                            lo = 128 + VD * a
                            wv = w[:, :, 128 + V0 * a:128 + V0 * (a + 1)].unsqueeze(2).broadcast_to([128, QT, NC, V0])
                            ins = nc.vector.tensor_tensor(
                                pu[:, :, lo:lo + VD].rearrange("p j (c m) -> p j c m", c=NC), wv, xvec, ALU.mult)
                        ins.then_inc(p_prod, 1)

                    def columns(q):
                        return nc.values_load_multi_w_load_instructions(
                            base_i[0:1, bass.ds(q * QT, QT)], engines=[mybir.EngineType.DVE], min_val=0,
                            max_val=(N - 1) * AC, skip_runtime_bounds_check_because="base is clamped to [0, N)")[1]

                    def add_windows(q, u, cols, more=True):
                        dve.wait_ge(p_out, q + 1)
                        for j in range(QT):
                            if more:
                                selector(q + 2, u, j).then_inc(p_S, 1)
                            if not (isinstance(q, int) and q == 0 and j == 0):
                                dve.wait_ge(p_agg, q * QT + j)
                            a = agg[:, bass.ds(cols[j], WIN * AC)]
                            nc.vector.tensor_tensor(a, ps[:, 6 + u % 2, j * WIN * AC:(j + 1) * WIN * AC], a,
                                                    ALU.add).then_inc(p_agg, 1)

                    def step(i, u):
                        q = i * SLOTS + u
                        if isinstance(i, int) and q < 2:
                            for j in range(QT):
                                selector(q, u, j).then_inc(p_S, 1)
                        else:
                            add_windows(q - 2, u, columns(q - 2))
                        if isinstance(i, int) and q == NQ - 1:
                            rest = columns(q - 1), columns(q)
                        products(i, q, u)
                        if isinstance(i, int) and q == NQ - 1:
                            add_windows(q - 1, u - 1, rest[0], more=False)
                            add_windows(q, u, rest[1], more=False)
                    for u in range(SLOTS):
                        step(0, u)
                    with dve.Fori(1, NI - 1) as i:
                        for u in range(SLOTS):
                            step(i, u)
                    for u in range(SLOTS):
                        step(NI - 1, u)
                    dve.wait_ge(p_agg, NT)

                @block.tensor
                def _(pe):
                    def hidden(i, q, u):
                        pe.wait_ge(p_emb[u], (i + 1) * 16)
                        if not (isinstance(q, int) and q < 2):
                            pe.wait_ge(p_hid, q - 1)
                        nc.tensor.matmul(hid_ps(u), fc1_sb[:, :], emb[:, u, :], start=True,
                                         stop=True).then_inc(p_hidps, 1)

                    def weights(q, u):
                        pe.wait_ge(p_hid, q + 1)
                        if not (isinstance(q, int) and q < 2):
                            pe.wait_ge(p_prod, q - 1)
                        for j in range(QT):
                            ins = nc.tensor.matmul(w_ps(u)[:, j, 0:WN], hid[:, u % 2, j * TE:(j + 1) * TE],
                                                   fc2_sb[:, :], start=True, stop=True)
                        ins.then_inc(p_w, 1)

                    def put(oj, b, cols, w, sj, comps):
                        nc.tensor.matmul(oj[32 * b:32 * b + 32, :, cols], w, sj[:, :, comps],
                                         start=True, stop=True, tile_position=(0, 32 * b))

                    def scatter(q, u):
                        pe.wait_ge(p_prod, q + 1)
                        pe.wait_ge(p_S, q * QT + QT)
                        if not (isinstance(q, int) and q < 2):
                            pe.wait_ge(p_agg, q * QT - QT)
                        for j in range(QT):
                            pj, sj, oj = P[:, u % 2, j, :], S[:, u % 2, j, :, :], out_ps(u)[:, j, :, :]
                            vs, vv = pj[:, 128:128 + VD], pj[:, 128 + VD:128 + 2 * VD]
                            for b in range(2):
                                x0 = pj[:, 32 * b:32 * b + 32]
                                x1 = pj[:, 64 + 32 * b:96 + 32 * b]
                                put(oj, b, slice(0, 1), x0, sj, slice(0, 1))
                                put(oj, b, slice(1, 3), x1, sj, slice(1, 4, 2))
                                put(oj, 2 + b, slice(1, 2), x1, sj, slice(2, 3))
                            put(oj, 3, slice(0, 1), vs[:, 0:32], sj, slice(0, 1))
                            put(oj, 2, slice(2, 3), vs[:, 32:64], sj, slice(0, 1))
                            put(oj, 3, slice(2, 3), vs[:, 64:96], sj, slice(0, 1))
                            for c in range(NC):
                                ins = nc.tensor.matmul(oj[64:96, :, 0], vv[:, V0 * c:V0 * (c + 1)], sj[:, :, 1 + c],
                                                       start=(c == 0), stop=(c == NC - 1), tile_position=(0, 64))
                        ins.then_inc(p_out, 1)

                    def step(i, u):
                        q = i * SLOTS + u
                        first = isinstance(i, int) and i == 0
                        hidden(i, q, u)
                        if not (first and u < 1):
                            weights(q - 1, u - 1)
                        if not (first and u < 2):
                            scatter(q - 2, u)
                    def warm(n):
                        for _ in range(n):
                            nc.tensor.matmul(ps[:, 0, 0:WN], fc2_sb[:, 0:128], fc2_sb[:, :], start=True, stop=True)
                    for u in range(SLOTS):
                        if u == 2:
                            warm(WARM)
                        step(0, u)
                    with pe.Fori(1, NI) as i:
                        for u in range(SLOTS):
                            step(i, u)
                    weights(NQ - 1, SLOTS - 1)
                    warm(WARM_LAST // 2)
                    scatter(NQ - 2, 0)
                    warm(WARM_LAST)
                    scatter(NQ - 1, 1)
                    warm(WARM_END)

            nums = [s.num for s in pass_sems]
            assert max(nums) - min(nums) + 1 == len(nums)
            nc.gpsimd.dma_reset(range(min(nums), max(nums) + 1))
            nc.gpsimd.sem_clear(range(min(nums), max(nums) + 1))
            nc.all_engine_barrier()

        with nc.Fori(0, end, WIN):
            passes()

        e_ps, e_act, e_tot, e_res, e_xh, e_gate = (sem("e_" + n) for n in ("ps", "act", "tot", "res", "xh", "gate"))
        e_out = [sem(f"e_out{i}") for i in range(RES)]

        def o_ps(t):
            return ps[0:NTN, t % 4, 0:WN]

        with nc.Block() as block:
            @block.tensor
            def _(pe):
                for t in range(NN):
                    if t >= 4:
                        pe.wait_ge(e_tot, t - 3)
                    a = agg_v[:, t * NTN:(t + 1) * NTN, :]
                    o = o_ps(t)
                    nc.tensor.matmul(o[:, 0:128], a[:, :, 0], wo0[:, :], start=True, stop=False)
                    nc.tensor.matmul(o[:, 128:192], a[:, :, 2], wo2[:, :], start=False, stop=False)
                    ins = nc.tensor.matmul(o[:, 96:160], a[:, :, 1], wo1[:, :], start=False, stop=True)
                    ins.then_inc(e_ps, 1)

            @block.scalar
            def _(act):
                for t in range(NN):
                    act.wait_ge(e_tot, t + 1)
                    if t >= RES:
                        act.wait_ge(e_out[t % RES], 16 * (t // RES))
                    nc.scalar.activation(gates[:, t % 4, :], total[:, t % 4, S0:96], ACT.Silu)
                    nc.scalar.activation(res[:, t % RES, 0:S0], total[:, t % 4, 0:S0], ACT.Silu).then_inc(e_act, 1)

            @block.gpsimd
            def _(pool):
                for t in range(NN):
                    nc.gpsimd.tensor_tensor(x_sb[:, t, :], x_sb[:, t, :], h_sb[:, t, :], ALU.add).then_inc(e_xh, 1)

            @block.vector
            def _(dve):
                def with_own(t):
                    dve.wait_ge(e_ps, t + 1)
                    nc.vector.tensor_tensor(
                        total[:, t % 4, :].rearrange("p (a w) -> p a w", a=2), o_ps(t).rearrange("p (a w) -> p a w", a=2),
                        own(t), ALU.add).then_inc(e_tot, 1)

                def own(t):
                    return prod_flat[:, t * PW:t * PW + 2 * (96 + D)].rearrange("p (a w) -> p a w", a=2)[:, :, 0:96]

                def gated(t):
                    dve.wait_ge(e_act, t + 1)
                    g = gates[:, t % 4, :].unsqueeze(1).broadcast_to([NTN, NC, V0])
                    v = total[:, t % 4, 96:192].rearrange("p (c m) -> p c m", c=NC)
                    nc.vector.tensor_tensor(vec(res[:, t % RES, S0:D]), v, g, ALU.mult).then_inc(e_gate, 1)

                def residual(t):
                    dve.wait_ge(e_xh, t + 1)
                    dve.wait_ge(e_gate, t + 1)
                    r = res[:, t % RES, :]
                    nc.vector.tensor_tensor(r, r, x_sb[:, t, :], ALU.add).then_inc(e_res, 1)

                for t in range(NN + 2):
                    if t < NN:
                        with_own(t)
                    if 1 <= t < NN + 1:
                        gated(t - 1)
                    if t >= 2:
                        residual(t - 2)

            @block.sync
            def _(sp):
                for t in range(NN):
                    sp.wait_ge(e_res, t + 1)
                    sp.dma_start(outv[t], res[:, t % RES, :]).then_inc(e_out[t % RES], 16)
                for i in range(RES):
                    sp.wait_ge(e_out[i], 16 * len(range(i, NN, RES)))


def kernel(**inputs):
    import numpy as np
    import concourse.bacc as bacc
    from concourse.bass_utils import run_bass_kernel_spmd as run

    a = {k: np.asarray(v) for k, v in inputs.items()}
    pad = EP - E
    src = np.pad(a["src"], (0, pad), mode="edge")
    dst = np.pad(a["dst"], (0, pad), mode="edge")
    sh = np.pad(a["edge_attr_4"], ((0, pad + QT * TE), (0, 0)))
    emb = np.pad(a["edge_attr_8"], ((0, pad), (0, 0)))
    p = "L0_gnn_"
    arrays = {
        "x": a["x"],
        "src_t": src.reshape(NT, TE).T,
        "dst_t": dst.reshape(NT, TE).T,
        "dst_q": dst.reshape(NQ, QT, TE),
        "sh_t": sh.reshape(NT + QT, TE, 4).transpose(1, 0, 2),
        "emb_t": emb.T,
        "w1s": a[p + "W1_s"], "w1v": a[p + "W1_v"],
        "fc1": a[p + "fc_w1"], "fb1": a[p + "fc_b1"][:, None],
        "fc2": a[p + "fc_w2"], "fb2": a[p + "fc_b2"][None, :],
        "w2s": a[p + "W2_s"], "w2v": a[p + "W2_v"],
        "wscs": a[p + "Wsc_s"], "wscv": a[p + "Wsc_v"],
    }
    arrays = {k: np.ascontiguousarray(v) for k, v in arrays.items()}
    nc = bacc.Bacc("TRN2", target_bir_lowering=False, num_devices=1)
    aps = [nc.dram_tensor(k, v.shape, mybir.dt.from_np(v.dtype), kind="ExternalInput").ap() for k, v in arrays.items()]
    o = nc.dram_tensor("out", (N, D), F32, kind="ExternalOutput").ap()
    build(nc, *aps, o)
    r = run(nc, [arrays], core_ids=[0])
    return r.results[0]["out"]
```
